# Optimizing a Trainium2 kernel written in Bass

```python
import numpy as np
import jax
import jax.numpy as jnp

def _softmax(x, axis=-1):
    return jax.nn.softmax(x, axis=axis)

def _gelu(x):
    return jax.nn.gelu(x, approximate=True)

def _silu(x):
    return jax.nn.silu(x)

def _sigmoid(x):
    return jax.nn.sigmoid(x)

def _layernorm(x, axis=-1, eps=1e-05):
    m = jnp.mean(x, axis=axis, keepdims=True)
    v = jnp.var(x, axis=axis, keepdims=True)
    return (x - m) / jnp.sqrt(v + eps)

def _scatter_add(tgt, idx, src, axis=0):
    return tgt.at[idx].add(src)

def _segment_sum(src, seg, n):
    return jax.ops.segment_sum(src, seg, n)
kernel_name = 'mk_rec_standalone_d1_rec_r8_a882db'

def setup_inputs(seed: int=0):
    np.random.seed(seed)
    _w = jnp.asarray

    def _rec_inputs():
        import jax
        import jax.numpy as jnp
        _rk = jax.random.key(seed)
        r_x = jax.random.randint(jax.random.fold_in(_rk, 1), (2048, 24), 0, 1000, jnp.int32)
        return r_x
    r_x = _rec_inputs()

    def _L0_rec_setup():
        import jax, jax.numpy as jnp
        import numpy as np
        B, F, E, VOCAB = (1024, 24, 32, 1000)
        RED = max(1, F // 8)
        I_IDX, J_IDX = np.triu_indices(F, k=1)
        P = len(I_IDX)
        OFFSETS = np.concatenate([[0], np.cumsum([VOCAB] * F)[:-1]]).astype(np.int64)
        D_IN = F * (F - 1) * E
        MLP1, MLP2 = (64, 32)
        BN_EPS = 1e-05

        def _bilinear(t, bl_W, bl_b):
            vi = t[:, I_IDX, :]
            vj = t[:, J_IDX, :]
            p = (jnp.einsum('bpe,pef->bpf', vi, bl_W) + bl_b) * vj
            return p.reshape(t.shape[0], -1)

        def _bn_relu(h, g, b):
            mu = h.mean(axis=0)
            var = ((h - mu) ** 2).mean(axis=0)
            return jax.nn.relu((h - mu) * jax.lax.rsqrt(var + BN_EPS) * g + b)
        key = jax.random.key(seed)
        ks = jax.random.split(key, 16)
        s = lambda *sh: 1.0 / np.sqrt(sh[-1])
        return {'x': jax.random.randint(ks[0], (B, F), 0, VOCAB, dtype=jnp.int64), 'emb': jax.random.normal(ks[1], (F * VOCAB + 1, E), jnp.float32) * 0.05, 'se_w1': jax.random.normal(ks[2], (RED, F), jnp.float32) * s(RED, F), 'se_w2': jax.random.normal(ks[3], (F, RED), jnp.float32) * s(F, RED), 'bl_W': jax.random.normal(ks[4], (P, E, E), jnp.float32) * s(P, E, E), 'bl_b': jax.random.normal(ks[5], (P, E), jnp.float32) * 0.01, 'w1': jax.random.normal(ks[6], (D_IN, MLP1), jnp.float32) * s(D_IN, MLP1), 'b1': jnp.zeros((MLP1,), jnp.float32), 'g1': jnp.ones((MLP1,), jnp.float32), 'be1': jnp.zeros((MLP1,), jnp.float32), 'w2': jax.random.normal(ks[7], (MLP1, MLP2), jnp.float32) * s(MLP1, MLP2), 'b2': jnp.zeros((MLP2,), jnp.float32), 'g2': jnp.ones((MLP2,), jnp.float32), 'be2': jnp.zeros((MLP2,), jnp.float32), 'w3': jax.random.normal(ks[8], (MLP2, 1), jnp.float32) * s(MLP2, 1), 'b3': jnp.zeros((1,), jnp.float32)}
    _L0_rec_all = _L0_rec_setup()
    _L0_rec_in = {k: v for k, v in _L0_rec_all.items() if k in ('emb', 'se_w1', 'se_w2', 'bl_W', 'bl_b', 'w1', 'b1', 'g1', 'be1', 'w2', 'b2', 'g2', 'be2', 'w3', 'b3')}
    del _L0_rec_all
    return {'r_x': r_x, 'L0_rec_emb': _L0_rec_in['emb'], 'L0_rec_se_w1': _L0_rec_in['se_w1'], 'L0_rec_se_w2': _L0_rec_in['se_w2'], 'L0_rec_bl_W': _L0_rec_in['bl_W'], 'L0_rec_bl_b': _L0_rec_in['bl_b'], 'L0_rec_w1': _L0_rec_in['w1'], 'L0_rec_b1': _L0_rec_in['b1'], 'L0_rec_g1': _L0_rec_in['g1'], 'L0_rec_be1': _L0_rec_in['be1'], 'L0_rec_w2': _L0_rec_in['w2'], 'L0_rec_b2': _L0_rec_in['b2'], 'L0_rec_g2': _L0_rec_in['g2'], 'L0_rec_be2': _L0_rec_in['be2'], 'L0_rec_w3': _L0_rec_in['w3'], 'L0_rec_b3': _L0_rec_in['b3']}

def reference(r_x, L0_rec_emb, L0_rec_se_w1, L0_rec_se_w2, L0_rec_bl_W, L0_rec_bl_b, L0_rec_w1, L0_rec_b1, L0_rec_g1, L0_rec_be1, L0_rec_w2, L0_rec_b2, L0_rec_g2, L0_rec_be2, L0_rec_w3, L0_rec_b3):
    import jax
    import jax.numpy as jnp

    def _L0_rec_ref(x, emb, se_w1, se_w2, bl_W, bl_b, w1, b1, g1, be1, w2, b2, g2, be2, w3, b3):
        import jax, jax.numpy as jnp
        import numpy as np
        B, F, E, VOCAB = (1024, 24, 32, 1000)
        RED = max(1, F // 8)
        I_IDX, J_IDX = np.triu_indices(F, k=1)
        P = len(I_IDX)
        OFFSETS = np.concatenate([[0], np.cumsum([VOCAB] * F)[:-1]]).astype(np.int64)
        D_IN = F * (F - 1) * E
        MLP1, MLP2 = (64, 32)
        BN_EPS = 1e-05

        def _bilinear(t, bl_W, bl_b):
            vi = t[:, I_IDX, :]
            vj = t[:, J_IDX, :]
            p = (jnp.einsum('bpe,pef->bpf', vi, bl_W) + bl_b) * vj
            return p.reshape(t.shape[0], -1)

        def _bn_relu(h, g, b):
            mu = h.mean(axis=0)
            var = ((h - mu) ** 2).mean(axis=0)
            return jax.nn.relu((h - mu) * jax.lax.rsqrt(var + BN_EPS) * g + b)
        idx = x + jnp.asarray(OFFSETS)[None, :]
        e = emb[idx]
        z = e.mean(axis=2)
        a = jax.nn.relu(z @ se_w1.T)
        A = jax.nn.relu(a @ se_w2.T)
        v = e * A[:, :, None]
        concat_p = jnp.concatenate([_bilinear(e, bl_W, bl_b), _bilinear(v, bl_W, bl_b)], axis=1)
        h = _bn_relu(concat_p @ w1 + b1, g1, be1)
        h = _bn_relu(h @ w2 + b2, g2, be2)
        out = (h @ w3 + b3).squeeze(1)
        return jax.nn.sigmoid(out)
    y = _L0_rec_ref(r_x, L0_rec_emb, L0_rec_se_w1, L0_rec_se_w2, L0_rec_bl_W, L0_rec_bl_b, L0_rec_w1, L0_rec_b1, L0_rec_g1, L0_rec_be1, L0_rec_w2, L0_rec_b2, L0_rec_g2, L0_rec_be2, L0_rec_w3, L0_rec_b3)
    return y

_drawn_inputs = setup_inputs


def setup_inputs(seed=0):
    import zlib

    import numpy as np

    out = dict(_drawn_inputs(seed))
    spreads = {'L0_rec_b1': (0.0, 0.8),
     'L0_rec_g1': (1.0, 0.2),
     'L0_rec_be1': (0.0, 0.1),
     'L0_rec_b2': (0.0, 0.8),
     'L0_rec_g2': (1.0, 0.2),
     'L0_rec_be2': (0.0, 0.1)}
    factors = {'L0_rec_se_w1': 8.0, 'L0_rec_se_w2': 8.0}
    for name, (base, spread) in spreads.items():
        noise = np.random.default_rng([zlib.crc32(name.encode()), seed]).standard_normal(out[name].shape)
        drawn = base * np.exp(spread * noise) if base else spread * noise
        out[name] = jnp.asarray(drawn.astype(out[name].dtype))
    for name, factor in factors.items():
        out[name] = (out[name] * factor).astype(out[name].dtype)
    return out
```

```python
from contextlib import ExitStack

import concourse.bass as bass
from concourse import mybir

F32 = mybir.dt.float32
F32R = mybir.dt.float32r
I32 = mybir.dt.int32
ALU = mybir.AluOpType
ACT = mybir.ActivationFunctionType

PARTS = 128
FIELDS_PER_BLOCK = 4
STACK_SLOTS = 6
Q_SLOTS = 3
CB = 512
BN_EPS = 1e-5


def plan_groups(F):
    nb = F // FIELDS_PER_BLOCK
    first = [i * F - i * (i + 1) // 2 for i in range(F)]

    def pair(i, j):
        return first[i] + j - i - 1

    groups, placed, tiles = [], [], 0
    for I in range(nb):
        i0, i1, i2, i3 = range(4 * I, 4 * I + 4)
        for i in (i0, i1, i2, i3):
            for J in range(I + 1, nb):
                for q in range(4):
                    placed.append((pair(i, 4 * J + q), tiles, q, len(groups)))
                groups.append((J, [(i, tiles)], True))
                tiles += 1
        for q, j in ((1, i1), (2, i2), (3, i3)):
            placed.append((pair(i0, j), tiles, q, len(groups)))
        placed.append((pair(i1, i3), tiles + 1, 0, len(groups)))
        groups.append((I, [(i0, tiles), (i1, tiles + 1)], False))
        placed.append((pair(i1, i2), tiles + 2, 2, len(groups)))
        placed.append((pair(i2, i3), tiles + 3, 3, len(groups)))
        groups.append((I, [(i1, tiles + 2), (i2, tiles + 3)], False))
        tiles += 4
    return groups, placed, tiles


def runs(placed):
    out = []
    for p, t, q, g in placed:
        if out and out[-1][0] + out[-1][3] == p and out[-1][1] + out[-1][3] == 4 * t + q \
                and out[-1][2] + out[-1][3] == 4 * g + q:
            out[-1][3] += 1
        else:
            out.append([p, 4 * t + q, 4 * g + q, 1])
    return out


def build(nc, x, emb, se_w1, se_w2, bl_W, bl_b, w1, b1, g1, be1, w2, b2, g2, be2, w3, b3, out):
    B, F = x.shape
    rows, E = emb.shape
    vocab = (rows - 1) // F
    npairs = bl_W.shape[0]
    R = se_w1.shape[0]
    M1, M2 = w2.shape
    NB = F // FIELDS_PER_BLOCK
    NCH = B // CB
    TB = CB // PARTS
    assert E * FIELDS_PER_BLOCK == PARTS and npairs == F * (F - 1) // 2 and M1 == 64 and B % CB == 0

    groups, placed, NT = plan_groups(F)
    NG = len(groups)
    spans = runs(placed)
    users = sorted({i for _, parts, _ in groups for i, _ in parts})
    per_slot = [len([i for i in users if i % STACK_SLOTS == s]) for s in range(STACK_SLOTS)]
    last_of_field = {i: max(g for g, (_, parts, _) in enumerate(groups) if i in [a for a, _ in parts]) for i in users}
    last_full_of_block = {J: max([g for g, (b, _, f) in enumerate(groups) if b == J and f], default=None)
                          for J in range(NB)}
    last_of_block = {J: max(g for g, (b, _, _) in enumerate(groups) if b == J) for J in range(NB)}
    first_of_block = {I: min(g for g, (_, parts, _) in enumerate(groups) if parts[0][0] // 4 == I) for I in range(NB)}

    with ExitStack() as ctx:
        def sb(name, shape, dt=F32):
            return ctx.enter_context(nc.sbuf_tensor(name, shape, dt))

        def ps(name, shape, dt=F32):
            return ctx.enter_context(nc.psum_tensor(name, shape, dt))

        def sem(name):
            return ctx.enter_context(nc.semaphore(name))

        pairW = sb("pairW", [PARTS, NT * PARTS], F32R)
        mlpW = sb("mlpW", [PARTS, NG, 2, M1])
        pair_bias = sb("pair_bias", [PARTS, NG])
        gate_down = sb("gate_down", [PARTS, NB, R])
        gate_up = sb("gate_up", [PARTS, F, E])
        gate_up_raw = sb("gate_up_raw", [R, F])
        bias_rows = sb("bias_rows", [NG, PARTS])
        ident = sb("ident", [PARTS, PARTS])
        fold = sb("fold", [PARTS, M1])
        w2s = sb("w2s", [M1, M2])
        w3s = sb("w3s", [M2, 1])
        vec1 = sb("vec1", [PARTS, 3])
        vec2 = sb("vec2", [M2, 3])
        b3s = sb("b3s", [1, 1])
        EV_COLS = 2 * NB * CB
        work = sb("work", [PARTS, EV_COLS + B + Q_SLOTS * 2 * CB])
        raw = work[:, 0:npairs * E]
        EV = work[:, 0:EV_COLS].rearrange("p (s j b) -> p s j b", s=2, j=NB)
        H = work[:, EV_COLS:EV_COLS + B]
        Q = work[:, EV_COLS + B:EV_COLS + B + Q_SLOTS * 2 * CB].rearrange("p (k s b) -> p k s b", k=Q_SLOTS, s=2)
        EVnext = sb("EVnext", [PARTS, 2, NB, CB])
        HL = sb("HL", [PARTS, 2, 2, 2, CB], F32R)
        stack = sb("stack", [PARTS, STACK_SLOTS, 2, CB], F32R)
        nat = sb("nat", [PARTS, TB, F * E])
        aT = sb("aT", [PARTS, CB])
        xs = sb("xs", [PARTS, B // PARTS, F], I32)
        field_base = sb("field_base", [PARTS, TB, F], I32)
        idx = sb("idx", [PARTS, TB, F], I32)
        stats1 = sb("stats1", [M1, NCH, 6])
        stats2 = sb("stats2", [M2, NCH, 6])
        bn = sb("bn", [M1, 2, 8])
        act1 = nat[0:M1, :, :].rearrange("p t c -> p (t c)")[:, 0:B]
        lin2 = EVnext[0:M2].rearrange("p s j b -> p (s j b)")[:, 0:B]
        act2 = EVnext[0:M2].rearrange("p s j b -> p (s j b)")[:, B:2 * B]
        probs = EVnext[0:1].rearrange("p s j b -> p (s j b)")[:, 2 * B:3 * B]

        Y = [ps(f"Y{k}", [PARTS, 2, CB]) for k in range(2)]
        acc = ps("acc", [PARTS, CB])
        T = [ps(f"T{k}", [PARTS, CB]) for k in range(2)]
        gate = ps("gate", [PARTS, CB])

        names = ("x_in base_done idx_done idx_seen w_in w_spread ident_clear mlpW_clear vec1_clear aT_clear up_clear pairW_clear hi_w pairW_ready mlpW_in mlpW_in2 bias_in bias_T "
                 "bias_ready small_in small_in2 ident_done fold_ready up_ready t_done en_ready z_done a_ready b_done vn_ready "
                 "hi_ready lo_ready y_done q_done q_free acc_free folded stat1 norm1 sd1 act1_done lin2_done lin2_ready "
                 "stat2 norm2 sd2 act2_done out_lin prob_done stored").split()
        S = {n: sem(n) for n in names}
        (x_in, base_done, idx_done, idx_seen, w_in, w_spread, ident_clear, mlpW_clear, vec1_clear, aT_clear, up_clear,
         pairW_clear, hi_w, pairW_ready, mlpW_in, mlpW_in2, bias_in, bias_T,
         bias_ready, small_in, small_in2, ident_done, fold_ready, up_ready, t_done, en_ready, z_done, a_ready, b_done, vn_ready,
         hi_ready, lo_ready, y_done, q_done, q_free, acc_free, folded, stat1, norm1, sd1, act1_done, lin2_done,
         lin2_ready, stat2, norm2, sd2, act2_done, out_lin, prob_done, stored) = [S[n] for n in names]
        gathered = [sem(f"gathered{t}") for t in range(TB)]
        ev_in = [sem(f"ev_in{J}") for J in range(NB)]
        stack_in = [sem(f"stack_in{s}") for s in range(STACK_SLOTS)]

        def stack_landed(i, n):
            return (n * per_slot[i % STACK_SLOTS] + i // STACK_SLOTS + 1) * 64

        N_GATE_LOADS = FIELDS_PER_BLOCK * NB + 1
        N_MLP_LOADS = 9
        y_groups = [g for g, (_, parts, _) in enumerate(groups) if len(parts) == 2 and parts[0][0] % 4 == 1]
        xv = x.rearrange("(t p) f -> p t f", p=PARTS)
        w1v = w1.rearrange("(a r) m -> a r m", a=2)
        block = ctx.enter_context(nc.Block())

        def load_span(eng, span, landed):
            p, _, slot, n = span
            g, q = slot // 4, slot % 4
            count = 0
            for a in range(2):
                if n % 4 == 0:
                    src = w1v[a, p * E:(p + n) * E, :].rearrange("(t r) m -> r t m", r=PARTS)
                    eng.dma_start(mlpW[:, g:g + n // 4, a, :], src).then_inc(landed, 16)
                else:
                    eng.dma_start(mlpW[q * E:(q + n) * E, g, a, :], w1v[a, p * E:(p + n) * E, :]).then_inc(landed, 16)
                count += 1
            if n % 4 == 0:
                eng.dma_start(bias_rows[g:g + n // 4, :], bl_b[p:p + n, :].rearrange("(t q) f -> t (q f)", q=4)
                              ).then_inc(bias_in, 16)
            else:
                eng.dma_start(bias_rows[g:g + 1, q * E:(q + n) * E],
                              bl_b[p:p + n, :].rearrange("(o q) f -> o (q f)", o=1)).then_inc(bias_in, 16)
            return count

        sp_spans, act_spans = spans[0::2], spans[1::2]

        @block.sync
        def _(sp):
            sp.dma_start(xs[:], xv).then_inc(x_in, 16)
            with nc.allow_non_contiguous_dma(reason="rows of 32 values of the pair weights"):
                sp.dma_start(raw[0:E, :].rearrange("e (p f) -> e p f", f=E),
                             bl_W.rearrange("p e f -> e p f")).then_inc(w_in, 16)
            sp.wait_ge(mlpW_clear, len(y_groups) + 1)
            for span in sp_spans:
                load_span(sp, span, mlpW_in)
            sp.wait_ge(w_in, 16)
            sp.dma_start(raw[E:2 * E, :], raw[0:E, :]).then_inc(w_spread, 16)
            sp.wait_ge(w_spread, 16)
            sp.dma_start(raw[2 * E:4 * E, :], raw[0:2 * E, :]).then_inc(w_spread, 16)

            def value(v):
                return v if isinstance(v, int) else sp.to_reg(v)

            def swap(J, n):
                landed = value(n * 32 + 16)
                split = value(n * (2 * NB) + 2 * J + 2)
                read = value(n * NG + (last_full_of_block[J] or 0) + 1)
                sp.wait_ge(ev_in[J], landed)
                if J >= 2:
                    sp.wait_ge(lo_ready, split)
                if last_full_of_block[J] is not None:
                    sp.wait_ge(q_done, read)
                sp.dma_start(EV[0:E, :, J, :], EV[3 * E:4 * E, :, J, :]).then_inc(ev_in[J], 16)

            def feed(n, is_first):
                def take(J):
                    made = value(n * NB + J + 1)
                    read = value((n - 1) * NG + last_of_block[J] + 1)
                    sp.wait_ge(vn_ready, made)
                    if not is_first:
                        sp.wait_ge(q_done, read)
                    sp.dma_start(EV[:, :, J, :], EVnext[:, :, J, :]).then_inc(ev_in[J], 16)

                def build_stack(i):
                    I, r, slot = i // 4, i % 4, i % STACK_SLOTS
                    split = value(n * (2 * NB) + 2 * I + 2)
                    held = [k for k in users if k % STACK_SLOTS == slot and k < i]
                    if held:
                        through = value(n * NG + last_of_field[held[-1]] + 1)
                    elif not is_first:
                        k = max(k for k in users if k % STACK_SLOTS == slot)
                        through = value((n - 1) * NG + last_of_field[k] + 1)
                    sp.wait_ge(lo_ready, split)
                    if held or not is_first:
                        sp.wait_ge(y_done, through)
                    for q in range(4):
                        sp.dma_start(stack[q * E:(q + 1) * E, slot, :, :].bitcast(F32),
                                     HL[r * E:(r + 1) * E, I % 2, :, q % 2, :].bitcast(F32)).then_inc(stack_in[slot], 16)

                if is_first:
                    sp.wait_ge(pairW_ready, 1)
                take(1)
                build_stack(0)
                for J in range(2, NB):
                    take(J)
                build_stack(1)
                take(0)
                swap(0, n)
                for i in users[2:]:
                    if i % 4 == 2 and i > 4 and i // 4 < NB:
                        swap(i // 4, n)
                    build_stack(i)

            feed(0, True)
            with sp.Fori(1, NCH) as n:
                feed(n, False)
            sp.wait_ge(prob_done, NCH)
            sp.dma_start(out.rearrange("(o b) -> o b", o=1), probs).then_inc(stored, 16)
            sp.wait_ge(stored, 16)

        @block.gpsimd
        def _(pool):
            nc.gpsimd.iota(field_base[:], pattern=[[0, TB], [vocab, F]], base=0, channel_multiplier=0
                           ).then_inc(base_done, 1)
            pool.wait_ge(ident_clear, 1)
            nc.gpsimd.affine_select(out=ident[:], in_=ident[:], compare_op=ALU.not_equal, fill=1.0, base=0,
                                    pattern=[[-1, PARTS]], channel_multiplier=1).then_inc(ident_done, 1)
            pool.wait_ge(base_done, 1)
            pool.wait_ge(x_in, 16)

            def gather(n, is_first):
                if not is_first:
                    for t in range(TB):
                        pool.wait_ge(gathered[t], n * (16 * F))
                    pool.wait_ge(t_done, n * NB)
                nc.gpsimd.tensor_tensor(idx[:], xs[:, bass.ds(n * TB, TB), :], field_base[:], ALU.add
                                        ).then_inc(idx_done, 1)
                pool.wait_ge(idx_done, n + 1)
                pool.sem_inc(idx_seen, 1)
                for t in range(TB):
                    for f in range(F):
                        nc.gpsimd.indirect_dma_start(
                            nat[:, t, f * E:(f + 1) * E], None, emb,
                            bass.IndirectOffsetOnAxis(ap=idx[:, t, f:f + 1], axis=0)).then_inc(gathered[t], 16)

            gather(0, True)
            with pool.Fori(1, NCH) as n:
                gather(n, False)

        PREP_T = NG - 26
        PREP_Z = PREP_T + NB + 1
        PREP_B = PREP_Z + 1
        PREP_S = [first_of_block[NB - 2] + 2, last_of_block[NB - 2] + 1]

        @block.tensor
        def _(pe):
            def transpose_block(J, n, is_first):
                if J == 0:
                    for t in range(TB):
                        pe.wait_ge(gathered[t], (n + 1) * (16 * F))
                if J >= 2:
                    pe.wait_ge(en_ready, n * NB + J - 1)
                elif not is_first:
                    pe.wait_ge(vn_ready, n * NB + J - 1)
                for t in range(TB):
                    mm = nc.tensor.transpose(T[J % 2][:, t * PARTS:(t + 1) * PARTS],
                                             nat[:, t, J * PARTS:(J + 1) * PARTS], ident[:])
                mm.then_inc(t_done, 1)

            def gate_hidden(n, is_first):
                pe.wait_ge(en_ready, n * NB + NB)
                if not is_first:
                    pe.wait_ge(a_ready, n)
                for J in range(NB):
                    mm = nc.tensor.matmul(gate[0:R, :], gate_down[:, J, :], EVnext[:, 0, J, :],
                                          start=(J == 0), stop=(J == NB - 1))
                mm.then_inc(z_done, 1)

            def gate_block(J, n):
                if J == 0:
                    pe.wait_ge(a_ready, n + 1)
                if J >= 2:
                    pe.wait_ge(vn_ready, n * NB + J - 1)
                nc.tensor.matmul(T[J % 2][:], gate_up[:, 4 * J:4 * J + 4, :].rearrange("p j e -> p (j e)"), aT[:],
                                 start=True, stop=True).then_inc(b_done, 1)

            def products(g, n, is_first=False):
                _, parts, _ = groups[g]
                for i, _ in parts:
                    pe.wait_ge(stack_in[i % STACK_SLOTS], stack_landed(i, n))
                if not is_first:
                    pe.wait_ge(q_done, n * NG + g - 1)
                for s in range(2):
                    for k, (i, tile) in enumerate(parts):
                        mm = nc.tensor.matmul(Y[g % 2][:, s, :], pairW[:, tile * PARTS:(tile + 1) * PARTS],
                                              stack[:, i % STACK_SLOTS, s, :],
                                              start=(k == 0), stop=(k == len(parts) - 1))
                mm.then_inc(y_done, 1)

            def contract(g, n):
                pe.wait_ge(q_done, n * NG + g + 1)
                if g == 0:
                    pe.wait_ge(acc_free, n + 1)
                for s in range(2):
                    mm = nc.tensor.matmul(acc[s * M1:(s + 1) * M1, :], mlpW[:, g, s, :], Q[:, g % Q_SLOTS, s, :],
                                          start=(g == 0), stop=(g == NG - 1))
                mm.then_inc(q_free, 1)

            def chunk(n, prepare):
                for g in range(NG):
                    if g + 2 < NG:
                        products(g + 2, n)
                    elif prepare:
                        products(g + 2 - NG, n + 1)
                    contract(g, n)
                    if prepare:
                        if PREP_T <= g < PREP_T + NB:
                            transpose_block(g - PREP_T, n + 1, False)
                        if g == PREP_Z:
                            gate_hidden(n + 1, False)
                        if PREP_B <= g < PREP_B + NB:
                            gate_block(g - PREP_B, n + 1)

            pe.sem_inc(q_free, Q_SLOTS)
            pe.sem_inc(acc_free, 1)
            pe.wait_ge(ident_done, 1)
            pe.wait_ge(bias_in, 16 * len(spans))
            nc.tensor.transpose(Y[0][:, 0, 0:NG], bias_rows[:], ident[0:NG, 0:NG]).then_inc(bias_T, 1)
            for J in range(NB):
                transpose_block(J, 0, True)
            pe.wait_ge(small_in, 16 * N_GATE_LOADS)
            gate_hidden(0, True)
            pe.wait_ge(up_ready, 1)
            for J in range(NB):
                gate_block(J, 0)
            pe.wait_ge(pairW_ready, 1)
            pe.wait_ge(bias_ready, 1)
            pe.wait_ge(mlpW_in, 16 * 2 * len(sp_spans))
            pe.wait_ge(mlpW_in2, 16 * 2 * len(act_spans))
            products(0, 0, True)
            products(1, 0, True)
            with pe.Fori(0, NCH - 1) as n:
                chunk(n, True)
            chunk(NCH - 1, False)

            banks = [Y[n // 2][:, n % 2, :] for n in range(NCH)]
            pe.wait_ge(acc_free, NCH + 1)
            pe.wait_ge(fold_ready, 2)
            pe.wait_ge(small_in2, 16 * N_MLP_LOADS)
            for n in range(NCH):
                nc.tensor.matmul(banks[n][0:M1, :], fold[:], H[:, n * CB:(n + 1) * CB],
                                 start=True, stop=True).then_inc(folded, 1)
            for n in range(NCH):
                pe.wait_ge(act1_done, n + 1)
                nc.tensor.matmul(banks[n][0:M2, :], w2s[:], act1[:, n * CB:(n + 1) * CB],
                                 start=True, stop=True).then_inc(lin2_done, 1)
            for n in range(NCH):
                pe.wait_ge(act2_done, n + 1)
                nc.tensor.matmul(banks[n][0:1, :], w3s[:], act2[:, n * CB:(n + 1) * CB],
                                 start=True, stop=True).then_inc(out_lin, 1)

        @block.scalar
        def _(act):
            small = [(vec1[0:M1, 0:1], b1), (vec1[0:M1, 1:2], g1), (vec1[0:M1, 2:3], be1),
                     (vec2[:, 0:1], b2), (vec2[:, 1:2], g2), (vec2[:, 2:3], be2), (b3s[:], b3)]
            with nc.allow_non_contiguous_dma(reason="small tables"):
                for q in range(4):
                    src = se_w1.rearrange("r (j q) -> q j r", q=4)[q:q + 1, :, :].to_broadcast([E, NB, R])
                    for J in range(NB):
                        act.dma_start(gate_down[q * E:(q + 1) * E, J, :], src[:, J, :]).then_inc(small_in, 16)
                act.dma_start(gate_up_raw[:], se_w2.rearrange("f r -> r f")).then_inc(small_in, 16)
                act.wait_ge(vec1_clear, 1)
                act.wait_ge(mlpW_clear, len(y_groups) + 1)
                for dst, src in small:
                    act.dma_start(dst, src.rearrange("(m o) -> m o", o=1)).then_inc(small_in2, 16)
                act.dma_start(w2s[:], w2).then_inc(small_in2, 16)
                act.dma_start(w3s[:], w3).then_inc(small_in2, 16)
            for span in act_spans:
                load_span(act, span, mlpW_in2)

            act.wait_ge(w_spread, 32)
            act.wait_ge(pairW_clear, NB)
            for k, (p, slot, _, n) in enumerate(spans):
                nc.scalar.copy(pairW[:, slot * E:(slot + n) * E], raw[:, p * E:(p + n) * E]).then_inc(hi_w, 1)

            def en(J, n, is_first):
                act.wait_ge(t_done, n * NB + J + 1)
                if not is_first:
                    act.wait_ge(ev_in[J], n * 32 - 16)
                    if J < 2:
                        act.wait_ge(lo_ready, (n - 1) * (2 * NB) + 2 * J + 2)
                nc.scalar.copy(EVnext[:, 0, J, :], T[J % 2][:]).then_inc(en_ready, 1)

            def hidden(n, is_first):
                act.wait_ge(z_done, n + 1)
                if not is_first:
                    act.wait_ge(b_done, n * NB)
                else:
                    act.wait_ge(aT_clear, 1)
                nc.scalar.activation(aT[0:R, :], gate[0:R, :], ACT.Relu, scale=1.0 / E).then_inc(a_ready, 1)

            def high(J, n, is_first):
                if J >= 2 or not is_first:
                    m, K = (n, J - 2) if J >= 2 else (n - 1, J - 2 + NB)
                    for i in users:
                        if i // 4 == K:
                            act.wait_ge(stack_in[i % STACK_SLOTS], stack_landed(i, m))
                if J < 2:
                    act.wait_ge(en_ready, n * NB + J + 1)
                    nc.scalar.copy(HL[:, J % 2, 0, 0, :], EVnext[:, 0, J, :]).then_inc(hi_ready, 1)
                    act.wait_ge(vn_ready, n * NB + J + 1)
                    nc.scalar.copy(HL[:, J % 2, 1, 0, :], EVnext[:, 1, J, :]).then_inc(hi_ready, 1)
                else:
                    act.wait_ge(ev_in[J], n * 32 + 16)
                    for s in range(2):
                        nc.scalar.copy(HL[:, J % 2, s, 0, :], EV[:, s, J, :]).then_inc(hi_ready, 1)

            def chunk(n, prepare):
                for g in range(NG):
                    for I in range(2, NB):
                        if g == first_of_block[I - 1]:
                            high(I, n, False)
                    if prepare:
                        if PREP_T <= g < PREP_T + NB:
                            en(g - PREP_T, n + 1, False)
                        if g == PREP_Z:
                            hidden(n + 1, False)
                        if g in PREP_S:
                            high(PREP_S.index(g), n + 1, False)
                act.wait_ge(q_free, n * NG + NG + Q_SLOTS)
                nc.scalar.activation(H[:, bass.ds(n * CB, CB)], acc[:], ACT.Identity, bias=vec1[:, 0:1]
                                     ).then_inc(acc_free, 1)

            for J in range(NB):
                en(J, 0, True)
            hidden(0, True)
            high(0, 0, True)
            high(1, 0, True)
            act.wait_ge(small_in2, 16 * N_MLP_LOADS)
            with act.Fori(0, NCH - 1) as n:
                chunk(n, True)
            chunk(NCH - 1, False)

            banks = [Y[n // 2][:, n % 2, :] for n in range(NCH)]
            for layer, (stat, sd, width) in enumerate(((stat1, sd1, M1), (stat2, sd2, M2))):
                act.wait_ge(stat, NCH + 2)
                nc.scalar.activation(bn[0:width, layer, 3:4], bn[0:width, layer, 2:3], ACT.Sqrt).then_inc(sd, 1)
                if layer == 0:
                    act.wait_ge(norm1, 4)
                    for n in range(NCH):
                        nc.scalar.activation(act1[:, n * CB:(n + 1) * CB], banks[n][0:M1, :], ACT.Relu,
                                             scale=bn[0:M1, 0, 5:6], bias=bn[0:M1, 0, 7:8]).then_inc(act1_done, 1)
                else:
                    act.wait_ge(norm2, 4)
                    for n in range(NCH):
                        nc.scalar.activation(act2[:, n * CB:(n + 1) * CB], lin2[:, n * CB:(n + 1) * CB], ACT.Relu,
                                             scale=bn[0:M2, 1, 5:6], bias=bn[0:M2, 1, 7:8]).then_inc(act2_done, 1)
            for n in range(NCH):
                act.wait_ge(out_lin, n + 1)
                nc.scalar.activation(probs[:, n * CB:(n + 1) * CB], banks[n][0:1, :], ACT.Sigmoid, bias=b3s[:]
                                     ).then_inc(prob_done, 1)

        @block.vector
        def _(dve):
            for g in y_groups:
                nc.vector.memset(mlpW[0:2 * E, g, :, :], 0.0).then_inc(mlpW_clear, 1)
            nc.vector.memset(bias_rows[:], 0.0).then_inc(mlpW_clear, 1)
            nc.vector.memset(vec1[:], 0.0).then_inc(vec1_clear, 1)
            nc.vector.memset(ident[:], 0.0).then_inc(ident_clear, 1)
            nc.vector.memset(aT[:], 0.0).then_inc(aT_clear, 1)
            nc.vector.memset(gate_up[:], 0.0).then_inc(up_clear, 1)
            for I in range(NB):
                tile = groups[last_of_block[I] - 1][1][0][1]
                nc.vector.memset(pairW[:, tile * PARTS:(tile + 4) * PARTS].bitcast(F32), 0.0).then_inc(pairW_clear, 1)
            dve.wait_ge(small_in, 16 * N_GATE_LOADS)
            dve.wait_ge(up_clear, 1)
            nc.vector.tensor_copy(gate_up[0:R, :, :], gate_up_raw[:].unsqueeze(2).to_broadcast([R, F, E])
                                  ).then_inc(up_ready, 1)
            dve.wait_ge(ident_done, 1)
            for a in range(2):
                nc.vector.tensor_copy(fold[a * M1:(a + 1) * M1, :], ident[a * M1:(a + 1) * M1, a * M1:(a + 1) * M1]
                                      ).then_inc(fold_ready, 1)
            for k, (p, slot, _, n) in enumerate(spans):
                dve.wait_ge(hi_w, k + 1)
                cols = pairW[2 * E:4 * E, slot * E:(slot + n) * E]
                lo = nc.vector.tensor_tensor(cols, raw[2 * E:4 * E, p * E:(p + n) * E], cols.bitcast(F32),
                                             ALU.subtract)
            lo.then_inc(pairW_ready, 1)
            dve.wait_ge(bias_T, 1)
            nc.vector.tensor_copy(pair_bias[:], Y[0][:, 0, 0:NG]).then_inc(bias_ready, 1)

            def v(J, n):
                dve.wait_ge(b_done, n * NB + J + 1)
                nc.vector.scalar_tensor_tensor(out=EVnext[:, 1, J, :], in0=T[J % 2][:], scalar=0.0,
                                               in1=EVnext[:, 0, J, :], op0=ALU.max, op1=ALU.mult
                                               ).then_inc(vn_ready, 1)

            def low(J, n):
                whole = EVnext if J < 2 else EV
                for s in range(2):
                    dve.wait_ge(hi_ready, n * (2 * NB) + 2 * J + s + 1)
                    nc.vector.tensor_tensor(HL[:, J % 2, s, 1, :], whole[:, s, J, :],
                                            HL[:, J % 2, s, 0, :].bitcast(F32), ALU.subtract).then_inc(lo_ready, 1)

            def multiply(g, n):
                J, _, full = groups[g]
                if full and g == min(k for k, (b, _, f) in enumerate(groups) if b == J and f):
                    dve.wait_ge(ev_in[J], n * 32 + 16)
                elif not full and g == last_of_block[J] - 1:
                    dve.wait_ge(ev_in[J], n * 32 + 32)
                dve.wait_ge(y_done, n * NG + g + 1)
                dve.wait_ge(q_free, n * NG + g + 1)
                nc.vector.scalar_tensor_tensor(out=Q[:, g % Q_SLOTS, :, :], in0=Y[g % 2][:], scalar=pair_bias[:, g:g + 1],
                                               in1=EV[:, :, J, :], op0=ALU.add, op1=ALU.mult).then_inc(q_done, 1)

            def chunk(n, prepare):
                for g in range(NG):
                    for I in range(2, NB):
                        if g == first_of_block[I - 1]:
                            low(I, n)
                    multiply(g, n)
                    if prepare:
                        if PREP_B < g <= PREP_B + NB:
                            v(g - PREP_B - 1, n + 1)
                        if g in PREP_S:
                            low(PREP_S.index(g), n + 1)

            for J in range(NB):
                v(J, 0)
            low(0, 0)
            low(1, 0)
            dve.wait_ge(bias_ready, 1)
            with dve.Fori(0, NCH - 1) as n:
                chunk(n, True)
            chunk(NCH - 1, False)

            banks = [Y[n // 2][:, n % 2, :] for n in range(NCH)]
            dve.wait_ge(small_in2, 16 * N_MLP_LOADS)
            for layer, (stat, sd, norm, stats, vec, width) in enumerate((
                    (stat1, sd1, norm1, stats1, vec1, M1), (stat2, sd2, norm2, stats2, vec2, M2))):
                for n in range(NCH):
                    if layer == 0:
                        dve.wait_ge(folded, n + 1)
                        nc.vector.bn_stats(stats[:, n, :], banks[n][0:M1, :]).then_inc(stat, 1)
                    else:
                        dve.wait_ge(lin2_done, n + 1)
                        nc.vector.tensor_scalar(lin2[:, n * CB:(n + 1) * CB], banks[n][0:M2, :], vec2[:, 0:1], None,
                                                ALU.add).then_inc(lin2_ready, 1)
                        dve.wait_ge(lin2_ready, n + 1)
                        nc.vector.bn_stats(stats[:, n, :], lin2[:, n * CB:(n + 1) * CB]).then_inc(stat, 1)
                col = [bn[0:width, layer, k:k + 1] for k in range(8)]
                dve.wait_ge(stat, NCH)
                nc.vector.bn_aggr(bn[0:width, layer, 0:2], stats[:].rearrange("p n k -> p (n k)")).then_inc(stat, 1)
                dve.wait_ge(stat, NCH + 1)
                nc.vector.tensor_scalar(col[2], col[1], BN_EPS, None, ALU.add).then_inc(stat, 1)
                dve.wait_ge(sd, 1)
                nc.vector.reciprocal(col[4], col[3]).then_inc(norm, 1)
                dve.wait_ge(norm, 1)
                nc.vector.tensor_tensor(col[5], col[4], vec[0:width, 1:2], ALU.mult).then_inc(norm, 1)
                dve.wait_ge(norm, 2)
                nc.vector.tensor_tensor(col[6], col[5], col[0], ALU.mult).then_inc(norm, 1)
                dve.wait_ge(norm, 3)
                nc.vector.tensor_tensor(col[7], vec[0:width, 2:3], col[6], ALU.subtract).then_inc(norm, 1)


_NAMES = ["x", "emb", "se_w1", "se_w2", "bl_W", "bl_b", "w1", "b1", "g1", "be1", "w2", "b2", "g2", "be2", "w3", "b3"]


def kernel(**inputs):
    import numpy as np
    import concourse.bacc as bacc
    from concourse.bass_utils import run_bass_kernel_spmd

    nc = bacc.Bacc("TRN2", target_bir_lowering=False, num_devices=1)
    arrays, args = {}, []
    for name in _NAMES:
        a = np.ascontiguousarray(inputs["r_x" if name == "x" else f"L0_rec_{name}"])
        arrays[f"in_{name}"] = a
        args.append(nc.dram_tensor(f"in_{name}", a.shape, mybir.dt.from_np(a.dtype), kind="ExternalInput").ap())
    out = nc.dram_tensor("out_prob", (arrays["in_x"].shape[0],), F32, kind="ExternalOutput").ap()
    build(nc, *args, out)
    r = run_bass_kernel_spmd(nc, [arrays], core_ids=[0])
    return r.results[0]["out_prob"]
```

```python
from contextlib import ExitStack

import concourse.bass as bass
from concourse import mybir

F32 = mybir.dt.float32
F32R = mybir.dt.float32r
I32 = mybir.dt.int32
ALU = mybir.AluOpType
ACT = mybir.ActivationFunctionType

PARTS = 128
FIELDS_PER_BLOCK = 4
STACK_SLOTS = 6
Q_SLOTS = 3
Y_SLOTS = 3
W_PIECES = 4
MLP_PIECES = 2
ROWS_AT, ROWS_APART = 55, 0
HIDDEN_AT = 59
GATES_AT, GATES_APART = 63, 1
FIRST_SPLIT_AT = 66
SPLIT_AT = {6: 1, 22: 2, 35: 3, 43: 4, 54: 5}
HIGH_LEAD = 6
CB = 512
BN_EPS = 1e-5


def plan_groups(F):
    nb = F // FIELDS_PER_BLOCK
    first = [i * F - i * (i + 1) // 2 for i in range(F)]

    def pair(i, j):
        return first[i] + j - i - 1

    groups, placed, tiles = [], [], 0
    def full_groups(i):
        nonlocal tiles
        for J in range(i // 4 + 1, nb):
            for q in range(4):
                placed.append((pair(i, 4 * J + q), tiles, q, len(groups)))
            groups.append((J, [(i, tiles)], True))
            tiles += 1

    for I in range(nb):
        i0, i1, i2, i3 = range(4 * I, 4 * I + 4)
        full_groups(i0)
        full_groups(i1)
        x_at = len(groups)
        groups.append((I, [(i0, tiles), (i1, tiles + 1)], False))
        first_tile, tiles = tiles, tiles + 4
        full_groups(i2)
        y_at = len(groups)
        groups.append((I, [(i1, first_tile + 2), (i2, first_tile + 3)], False))
        full_groups(i3)
        for q, j in ((1, i1), (2, i2), (3, i3)):
            placed.append((pair(i0, j), first_tile, q, x_at))
        placed.append((pair(i1, i3), first_tile + 1, 0, x_at))
        placed.append((pair(i1, i2), first_tile + 2, 2, y_at))
        placed.append((pair(i2, i3), first_tile + 3, 3, y_at))
    return groups, placed, tiles


def lay_out(F, E, bl_W, bl_b, w1, se_w1, se_w2, b1, g1, be1, b2, g2, be2, w3, b3):
    import numpy as np

    groups, placed, tiles = plan_groups(F)
    M1, M2 = w1.shape[1], w3.shape[0]
    R = se_w1.shape[0]
    pair_weights = np.zeros((E, 4 * tiles, E), bl_W.dtype)
    mlp_weights = np.zeros((4, E, len(groups), 2, M1), w1.dtype)
    biases = np.zeros((4, E, len(groups)), bl_b.dtype)
    w1_of_pair = w1.reshape(2, -1, E, M1)
    for p, tile, q, g in placed:
        pair_weights[:, 4 * tile + q, :] = bl_W[p]
        mlp_weights[q, :, g, :, :] = w1_of_pair[:, p].transpose(1, 0, 2)
        biases[q, :, g] = bl_b[p]
    down = np.repeat(se_w1.T.reshape(-1, 4, R).transpose(1, 0, 2), E, axis=0)
    up = np.zeros((4, E, F * E), se_w2.dtype)
    up[:, 0:R, :] = np.repeat(se_w2.T, E, axis=1)
    vectors1 = np.zeros((PARTS, 3), b1.dtype)
    vectors1[0:M1] = np.stack([b1, g1, be1], axis=1)
    vectors2 = np.zeros((M2, 5), b2.dtype)
    vectors2[:, 0:4] = np.stack([b2, g2, be2, w3[:, 0]], axis=1)
    vectors2[0, 4] = b3[0]
    return {"pair_weights": pair_weights.reshape(E, -1), "mlp_weights": mlp_weights.reshape(PARTS, -1),
            "biases": biases.reshape(PARTS, -1), "down": down.reshape(PARTS, -1), "up": up.reshape(PARTS, -1),
            "vectors1": vectors1, "vectors2": vectors2}


def build(nc, x, emb, w2, pair_weights, mlp_weights, biases, down, up, vectors1, vectors2, out):
    B, F = x.shape
    rows, E = emb.shape
    vocab = (rows - 1) // F
    M1, M2 = w2.shape
    NB = F // FIELDS_PER_BLOCK
    R = down.shape[1] // NB
    NCH = B // CB
    TB = CB // PARTS
    assert E * FIELDS_PER_BLOCK == PARTS and M1 == 64 and B % CB == 0

    groups, _, NT = plan_groups(F)
    NG = len(groups)
    NPAIR = NB // 2
    plain_steps = [("group", g) for g in range(NG)]
    full_steps = []
    for g in range(NG):
        full_steps += [("rows", k) for k in range(NPAIR) if g == ROWS_AT + k * ROWS_APART]
        full_steps += [("gates", k) for k in range(NPAIR) if g == GATES_AT + k * GATES_APART]
        full_steps.append(("group", g))
    assert len(full_steps) % Y_SLOTS == 0 and NG % Y_SLOTS == 0 and NG % Q_SLOTS == 0
    users = sorted({i for _, parts, _ in groups for i, _ in parts})
    slot_of = {i: k % STACK_SLOTS for k, i in enumerate(users)}
    per_slot = [len(users[s::STACK_SLOTS]) for s in range(STACK_SLOTS)]
    last_of_field = {i: max(g for g, (_, parts, _) in enumerate(groups) if i in [a for a, _ in parts]) for i in users}
    last_full_of_block = {J: max([g for g, (b, _, f) in enumerate(groups) if b == J and f], default=None)
                          for J in range(NB)}
    last_of_block = {J: max(g for g, (b, _, _) in enumerate(groups) if b == J) for J in range(NB)}
    first_of_field = {i: min(g for g, (_, parts, _) in enumerate(groups) if i in [a for a, _ in parts]) for i in users}

    with ExitStack() as ctx:
        def sb(name, shape, dt=F32):
            return ctx.enter_context(nc.sbuf_tensor(name, shape, dt))

        def ps(name, shape, dt=F32):
            return ctx.enter_context(nc.psum_tensor(name, shape, dt))

        def sem(name):
            return ctx.enter_context(nc.semaphore(name))

        pairW = sb("pairW", [PARTS, NT * PARTS], F32R)
        mlpW = sb("mlpW", [PARTS, NG, 2, M1])
        pair_bias = sb("pair_bias", [PARTS, NG])
        gate_down = sb("gate_down", [PARTS, NB, R])
        gate_up = sb("gate_up", [PARTS, F * E], F32R)
        ident = sb("ident", [PARTS, PARTS])
        fold = sb("fold", [PARTS, M1])
        w2s = sb("w2s", [M1, M2])
        vec1 = sb("vec1", [PARTS, 3])
        vec2 = sb("vec2", [M2, 5])
        w3s, b3s = vec2[:, 3:4], vec2[0:1, 4:5]
        EV_COLS = 2 * NB * CB
        work = sb("work", [PARTS, EV_COLS + B + Q_SLOTS * 2 * CB])
        raw = work[:, 0:NT * PARTS]
        EV = work[:, 0:EV_COLS].rearrange("p (s j b) -> p s j b", s=2, j=NB)
        H = work[:, EV_COLS:EV_COLS + B]
        Q = work[:, EV_COLS + B:EV_COLS + B + Q_SLOTS * 2 * CB].rearrange("p (k s b) -> p k s b", k=Q_SLOTS, s=2)
        EVnext = sb("EVnext", [PARTS, 2, NB, CB])
        HL = sb("HL", [PARTS, 2, 2, 2, CB], F32R)
        stack = sb("stack", [PARTS, STACK_SLOTS, 2, CB], F32R)
        nat = sb("nat", [PARTS, TB, F * E])
        a_stack = sb("a_stack", [PARTS, CB], F32R)
        up_raw = EVnext[:, 1, :, :].rearrange("p j b -> p (j b)")[:, 0:F * E]
        xs = sb("xs", [PARTS, B // PARTS, F], I32)
        field_base = sb("field_base", [PARTS, TB, F], I32)
        idx = sb("idx", [PARTS, TB, F], I32)
        stats1 = sb("stats1", [M1, NCH, 6])
        stats2 = sb("stats2", [M2, NCH, 6])
        bn = sb("bn", [M1, 2, 8])
        act1 = nat[0:M1, :, :].rearrange("p t c -> p (t c)")[:, 0:B]
        lin2 = EVnext[0:M2].rearrange("p s j b -> p (s j b)")[:, 0:B]
        act2 = EVnext[0:M2].rearrange("p s j b -> p (s j b)")[:, B:2 * B]
        probs = EVnext[0:1].rearrange("p s j b -> p (s j b)")[:, 2 * B:3 * B]

        Y = [ps(f"Y{k}", [PARTS, 2, CB]) for k in range(Y_SLOTS)]
        acc = ps("acc", [PARTS, CB])
        gate = ps("gate", [PARTS, CB])[0:R, :]

        names = ("x_in base_done idx_done idx_seen ident_clear ident_done fold_ready a_clear up_in hi_up up_ready "
                 "down_in hi_w pairW_ready mlpW_in bias_in vectors_in t_done en_ready z_done a_ready a_split b_done vn_ready "
                 "hi_ready lo_ready y_done q_done q_free acc_free folded stat1 norm1 sd1 act1_done lin2_done lin2_ready "
                 "stat2 norm2 sd2 act2_done out_lin prob_done stored").split()
        S = {n: sem(n) for n in names}
        (x_in, base_done, idx_done, idx_seen, ident_clear, ident_done, fold_ready, a_clear, up_in, hi_up, up_ready,
         down_in, hi_w, pairW_ready, mlpW_in, bias_in, vectors_in, t_done, en_ready, z_done, a_ready, a_split, b_done, vn_ready,
         hi_ready, lo_ready, y_done, q_done, q_free, acc_free, folded, stat1, norm1, sd1, act1_done, lin2_done,
         lin2_ready, stat2, norm2, sd2, act2_done, out_lin, prob_done, stored) = [S[n] for n in names]
        w_in = [sem(f"w_in{k}") for k in range(W_PIECES)]
        gathered = [sem(f"gathered{J}") for J in range(NB)]
        ev_in = [sem(f"ev_in{J}") for J in range(NB)]
        stack_in = [sem(f"stack_in{s}") for s in range(STACK_SLOTS)]

        def stack_landed(i, n):
            return (n * per_slot[slot_of[i]] + users.index(i) // STACK_SLOTS + 1) * 64

        W_COLS = NT * PARTS // W_PIECES
        xv = x.rearrange("(t p) f -> p t f", p=PARTS)
        block = ctx.enter_context(nc.Block())

        @block.sync
        def _(sp):
            sp.dma_start(xs[:], xv).then_inc(x_in, 16)
            sp.dma_start(up_raw, up).then_inc(up_in, 16)
            for k in range(W_PIECES):
                for q in range(4):
                    sp.dma_start(raw[q * E:(q + 1) * E, k * W_COLS:(k + 1) * W_COLS],
                                 pair_weights[:, k * W_COLS:(k + 1) * W_COLS]).then_inc(w_in[k], 16)
            sp.dma_start(gate_down[:].rearrange("p j r -> p (j r)"), down).then_inc(down_in, 16)
            sp.dma_start(pair_bias[:], biases).then_inc(bias_in, 16)
            mlpW_rows = mlpW[:].rearrange("p g a m -> p (g a m)")
            for k in range(MLP_PIECES):
                cols = slice(k * NG * 2 * M1 // MLP_PIECES, (k + 1) * NG * 2 * M1 // MLP_PIECES)
                sp.dma_start(mlpW_rows[:, cols], mlp_weights[:, cols]).then_inc(mlpW_in, 16)
            sp.dma_start(vec1[:], vectors1).then_inc(vectors_in, 16)
            sp.dma_start(vec2[:], vectors2).then_inc(vectors_in, 16)
            sp.dma_start(w2s[:], w2).then_inc(vectors_in, 16)

            def value(v):
                return v if isinstance(v, int) else sp.to_reg(v)

            def swap(J, n):
                landed = value(n * 32 + 16)
                split = value(n * (2 * NB) + 2 * J + 2)
                read = value(n * NG + (last_full_of_block[J] or 0) + 1)
                sp.wait_ge(ev_in[J], landed)
                if J >= 1:
                    sp.wait_ge(lo_ready, split)
                if last_full_of_block[J] is not None:
                    sp.wait_ge(q_done, read)
                sp.dma_start(EV[0:E, :, J, :], EV[3 * E:4 * E, :, J, :]).then_inc(ev_in[J], 16)

            def feed(n, is_first):
                def take(J):
                    made = value(n * NPAIR + J // 2 + 1)
                    read = value((n - 1) * NG + last_of_block[J] + 1)
                    sp.wait_ge(vn_ready, made)
                    if not is_first:
                        sp.wait_ge(q_done, read)
                    sp.dma_start(EV[:, :, J, :], EVnext[:, :, J, :]).then_inc(ev_in[J], 16)

                def build_stack(i):
                    I, r, slot = i // 4, i % 4, slot_of[i]
                    split = value(n * (2 * NB) + 2 * I + 2)
                    sharing = users[slot::STACK_SLOTS]
                    k = sharing.index(i)
                    if k:
                        through = value(n * NG + last_of_field[sharing[k - 1]] + 1)
                    elif not is_first:
                        through = value((n - 1) * NG + last_of_field[sharing[-1]] + 1)
                    sp.wait_ge(lo_ready, split)
                    if k or not is_first:
                        sp.wait_ge(y_done, through)
                    for q in range(4):
                        sp.dma_start(stack[q * E:(q + 1) * E, slot, :, :].bitcast(F32),
                                     HL[r * E:(r + 1) * E, I % 2, :, q % 2, :].bitcast(F32)).then_inc(stack_in[slot], 16)

                if is_first:
                    sp.wait_ge(pairW_ready, W_PIECES)
                build_stack(users[0])
                take(1)
                if not is_first:
                    swap(NB - 1, n - 1)
                for J in range(2, NB):
                    take(J)
                build_stack(users[1])
                take(0)
                swap(0, n)
                later = [(last_of_field[users[k - STACK_SLOTS]] if k >= STACK_SLOTS else 0, build_stack, (i,))
                         for k, i in enumerate(users) if k >= 2]
                later += [(last_full_of_block[J], swap, (J, n)) for J in range(1, NB - 1)]
                for _, move, which in sorted(later, key=lambda m: m[0]):
                    move(*which)

            feed(0, True)
            with sp.Fori(1, NCH) as n:
                feed(n, False)
            swap(NB - 1, NCH - 1)
            sp.wait_ge(prob_done, NCH)
            sp.dma_start(out.rearrange("(o b) -> o b", o=1), probs).then_inc(stored, 16)
            sp.wait_ge(stored, 16)

        @block.gpsimd
        def _(pool):
            nc.gpsimd.iota(field_base[:], pattern=[[0, TB], [vocab, F]], base=0, channel_multiplier=0
                           ).then_inc(base_done, 1)
            pool.wait_ge(ident_clear, 1)
            nc.gpsimd.affine_select(out=ident[:], in_=ident[:], compare_op=ALU.not_equal, fill=1.0, base=0,
                                    pattern=[[-1, PARTS]], channel_multiplier=1).then_inc(ident_done, 1)
            pool.wait_ge(base_done, 1)
            pool.wait_ge(x_in, 16)

            def gather(n, is_first):
                if not is_first:
                    for J in range(NB):
                        pool.wait_ge(gathered[J], n * (16 * FIELDS_PER_BLOCK * TB))
                    pool.wait_ge(t_done, n * NPAIR)
                nc.gpsimd.tensor_tensor(idx[:], xs[:, bass.ds(n * TB, TB), :], field_base[:], ALU.add
                                        ).then_inc(idx_done, 1)
                pool.wait_ge(idx_done, n + 1)
                pool.sem_inc(idx_seen, 1)
                for J in range(NB):
                    for t in range(TB):
                        for f in range(FIELDS_PER_BLOCK * J, FIELDS_PER_BLOCK * (J + 1)):
                            nc.gpsimd.indirect_dma_start(
                                nat[:, t, f * E:(f + 1) * E], None, emb,
                                bass.IndirectOffsetOnAxis(ap=idx[:, t, f:f + 1], axis=0)).then_inc(gathered[J], 16)

            gather(0, True)
            with pool.Fori(1, NCH) as n:
                gather(n, False)

        @block.tensor
        def _(pe):
            def fill_rows(k, slot, n):
                for J in (2 * k, 2 * k + 1):
                    pe.wait_ge(gathered[J], (n + 1) * (16 * FIELDS_PER_BLOCK * TB))
                    for t in range(TB):
                        mm = nc.tensor.transpose(Y[slot][:, J % 2, t * PARTS:(t + 1) * PARTS],
                                                 nat[:, t, J * PARTS:(J + 1) * PARTS], ident[:])
                mm.then_inc(t_done, 1)

            def gate_hidden(k, n, is_first):
                pe.wait_ge(en_ready, n * NPAIR + k + 1)
                if k == 0 and not is_first:
                    pe.wait_ge(a_ready, n)
                for J in (2 * k, 2 * k + 1):
                    mm = nc.tensor.matmul(gate, gate_down[:, J, :], EVnext[:, 0, J, :],
                                          start=(J == 0), stop=(J == NB - 1))
                if k == NPAIR - 1:
                    mm.then_inc(z_done, 1)

            def fill_gates(k, slot, n):
                if k == 0:
                    pe.wait_ge(a_split, 2 * n + 2)
                for J in (2 * k, 2 * k + 1):
                    mm = nc.tensor.matmul(Y[slot][:, J % 2, :], gate_up[:, J * PARTS:(J + 1) * PARTS], a_stack[:],
                                          start=True, stop=True)
                mm.then_inc(b_done, 1)

            def fill_products(g, slot, n):
                _, parts, _ = groups[g]
                for i, _ in parts:
                    if g == first_of_field[i]:
                        pe.wait_ge(stack_in[slot_of[i]], stack_landed(i, n))
                for s in range(2):
                    for k, (i, tile) in enumerate(parts):
                        mm = nc.tensor.matmul(Y[slot][:, s, :], pairW[:, tile * PARTS:(tile + 1) * PARTS],
                                              stack[:, slot_of[i], s, :],
                                              start=(k == 0), stop=(k == len(parts) - 1))
                mm.then_inc(y_done, 1)

            def contract(g, n):
                if g == 0:
                    pe.wait_ge(acc_free, n + 1)
                for s in range(2):
                    mm = nc.tensor.matmul(acc[s * M1:(s + 1) * M1, :], mlpW[:, g, s, :], Q[:, g % Q_SLOTS, s, :],
                                          start=(g == 0), stop=(g == NG - 1))
                mm.then_inc(q_free, 1)

            def chunk(n, steps, prepare):
                for c, (kind, k) in enumerate(steps):
                    if kind == "group":
                        pe.wait_ge(q_done, n * NG + k + 1)
                    elif kind == "rows":
                        pe.wait_ge(en_ready, (n + 1) * NPAIR + k + 1)
                    else:
                        pe.wait_ge(vn_ready, (n + 1) * NPAIR + k + 1)
                    slot, ahead = c % Y_SLOTS, c + Y_SLOTS
                    if ahead < len(steps):
                        kind_ahead, k_ahead = steps[ahead]
                        if kind_ahead == "group":
                            fill_products(k_ahead, slot, n)
                        elif kind_ahead == "rows":
                            fill_rows(k_ahead, slot, n + 1)
                        else:
                            fill_gates(k_ahead, slot, n + 1)
                    elif prepare:
                        fill_products(ahead - len(steps), slot, n + 1)
                    if kind == "group":
                        contract(k, n)
                    elif kind == "rows":
                        gate_hidden(k, n + 1, False)

            pe.sem_inc(q_free, Q_SLOTS)
            pe.sem_inc(acc_free, 1)
            pe.wait_ge(ident_done, 1)
            pe.wait_ge(down_in, 16)
            for k in range(NPAIR):
                fill_rows(k, k, 0)
                if k:
                    gate_hidden(k - 1, 0, True)
            gate_hidden(NPAIR - 1, 0, True)
            pe.wait_ge(up_ready, 2)
            for k in range(NPAIR):
                fill_gates(k, k, 0)
            pe.wait_ge(pairW_ready, W_PIECES)
            for k in range(NPAIR):
                pe.wait_ge(vn_ready, k + 1)
                fill_products(k, k, 0)
            pe.wait_ge(mlpW_in, 16 * MLP_PIECES)
            with pe.Fori(0, NCH - 1) as n:
                chunk(n, full_steps, True)
            chunk(NCH - 1, plain_steps, False)

            banks = [Y[n // 2][:, n % 2, :] for n in range(NCH)]
            pe.wait_ge(acc_free, NCH + 1)
            pe.wait_ge(fold_ready, 2)
            pe.wait_ge(vectors_in, 16 * 3)
            for n in range(NCH):
                nc.tensor.matmul(banks[n][0:M1, :], fold[:], H[:, n * CB:(n + 1) * CB],
                                 start=True, stop=True).then_inc(folded, 1)
            for n in range(NCH):
                pe.wait_ge(act1_done, n + 1)
                nc.tensor.matmul(banks[n][0:M2, :], w2s[:], act1[:, n * CB:(n + 1) * CB],
                                 start=True, stop=True).then_inc(lin2_done, 1)
            for n in range(NCH):
                pe.wait_ge(act2_done, n + 1)
                nc.tensor.matmul(banks[n][0:1, :], w3s, act2[:, n * CB:(n + 1) * CB],
                                 start=True, stop=True).then_inc(out_lin, 1)

        @block.scalar
        def _(act):
            act.wait_ge(up_in, 16)
            nc.scalar.copy(gate_up[:], up_raw).then_inc(hi_up, 1)
            for k in range(W_PIECES):
                act.wait_ge(w_in[k], 16 * 4)
                nc.scalar.copy(pairW[:, k * W_COLS:(k + 1) * W_COLS], raw[:, k * W_COLS:(k + 1) * W_COLS]
                               ).then_inc(hi_w, 1)

            def take_rows(k, slot, n, is_first):
                act.wait_ge(t_done, n * NPAIR + k + 1)
                if not is_first:
                    for J in (2 * k, 2 * k + 1):
                        act.wait_ge(ev_in[J], n * 32 - 16)
                    if k == 0:
                        act.wait_ge(lo_ready, (n - 1) * (2 * NB) + 2)
                nc.scalar.copy(EVnext[:, 0, 2 * k:2 * k + 2, :], Y[slot][:]).then_inc(en_ready, 1)

            def hidden(n, is_first):
                act.wait_ge(z_done, n + 1)
                if is_first:
                    act.wait_ge(pairW_ready, W_PIECES)
                    act.wait_ge(a_clear, 1)
                else:
                    act.wait_ge(b_done, n * NPAIR)
                for q in range(2):
                    nc.scalar.activation(a_stack[q * E:q * E + R, :], gate, ACT.Relu, scale=1.0 / E)
                nc.scalar.activation(H[0:R, bass.ds(n * CB, CB)], gate, ACT.Relu, scale=1.0 / E
                                     ).then_inc(a_ready, 1)

            def high(J, n):
                if J == 1:
                    act.wait_ge(y_done, n * NG + 1)
                elif J >= 2:
                    for i in users:
                        if i // 4 == J - 2:
                            act.wait_ge(stack_in[slot_of[i]], stack_landed(i, n))
                if J == 0:
                    act.wait_ge(en_ready, n * NPAIR + 1)
                    nc.scalar.copy(HL[:, J % 2, 0, 0, :], EVnext[:, 0, J, :]).then_inc(hi_ready, 1)
                    act.wait_ge(vn_ready, n * NPAIR + 1)
                    nc.scalar.copy(HL[:, J % 2, 1, 0, :], EVnext[:, 1, J, :]).then_inc(hi_ready, 1)
                else:
                    act.wait_ge(ev_in[J], n * 32 + 16)
                    for s in range(2):
                        nc.scalar.copy(HL[:, J % 2, s, 0, :], EV[:, s, J, :]).then_inc(hi_ready, 1)

            def chunk(n, steps, prepare):
                for c, (kind, k) in enumerate(steps):
                    if kind == "rows":
                        take_rows(k, c % Y_SLOTS, n + 1, False)
                    elif kind == "group":
                        for split, J in SPLIT_AT.items():
                            if k == max(0, split - HIGH_LEAD):
                                high(J, n)
                        if prepare and k == HIDDEN_AT:
                            hidden(n + 1, False)
                        if prepare and k == FIRST_SPLIT_AT:
                            for i in users:
                                if i // 4 == NB - 2:
                                    act.wait_ge(stack_in[slot_of[i]], stack_landed(i, n))
                            high(0, n + 1)
                act.wait_ge(q_free, n * NG + NG + Q_SLOTS)
                nc.scalar.activation(H[:, bass.ds(n * CB, CB)], acc[:], ACT.Identity, bias=vec1[:, 0:1]
                                     ).then_inc(acc_free, 1)

            for k in range(NPAIR):
                take_rows(k, k, 0, True)
            hidden(0, True)
            high(0, 0)
            act.wait_ge(vectors_in, 16 * 3)
            with act.Fori(0, NCH - 1) as n:
                chunk(n, full_steps, True)
            chunk(NCH - 1, plain_steps, False)

            banks = [Y[n // 2][:, n % 2, :] for n in range(NCH)]
            for layer, (stat, sd, width) in enumerate(((stat1, sd1, M1), (stat2, sd2, M2))):
                act.wait_ge(stat, NCH + 2)
                nc.scalar.activation(bn[0:width, layer, 3:4], bn[0:width, layer, 2:3], ACT.Sqrt).then_inc(sd, 1)
                if layer == 0:
                    act.wait_ge(norm1, 4)
                    for n in range(NCH):
                        nc.scalar.activation(act1[:, n * CB:(n + 1) * CB], banks[n][0:M1, :], ACT.Relu,
                                             scale=bn[0:M1, 0, 5:6], bias=bn[0:M1, 0, 7:8]).then_inc(act1_done, 1)
                else:
                    act.wait_ge(norm2, 4)
                    for n in range(NCH):
                        nc.scalar.activation(act2[:, n * CB:(n + 1) * CB], lin2[:, n * CB:(n + 1) * CB], ACT.Relu,
                                             scale=bn[0:M2, 1, 5:6], bias=bn[0:M2, 1, 7:8]).then_inc(act2_done, 1)
            for n in range(NCH):
                act.wait_ge(out_lin, n + 1)
                nc.scalar.activation(probs[:, n * CB:(n + 1) * CB], banks[n][0:1, :], ACT.Sigmoid, bias=b3s
                                     ).then_inc(prob_done, 1)

        @block.vector
        def _(dve):
            nc.vector.memset(ident[:], 0.0).then_inc(ident_clear, 1)
            nc.vector.memset(a_stack[:].bitcast(F32), 0.0).then_inc(a_clear, 1)
            dve.wait_ge(ident_done, 1)
            for a in range(2):
                nc.vector.tensor_copy(fold[a * M1:(a + 1) * M1, :], ident[a * M1:(a + 1) * M1, a * M1:(a + 1) * M1]
                                      ).then_inc(fold_ready, 1)
            dve.wait_ge(hi_up, 1)
            for q in (1, 3):
                rows = gate_up[q * E:(q + 1) * E, :]
                nc.vector.tensor_tensor(rows, up_raw[q * E:(q + 1) * E, :], rows.bitcast(F32), ALU.subtract
                                        ).then_inc(up_ready, 1)
            for k in range(W_PIECES):
                dve.wait_ge(hi_w, k + 1)
                cols = pairW[2 * E:4 * E, k * W_COLS:(k + 1) * W_COLS]
                nc.vector.tensor_tensor(cols, raw[2 * E:4 * E, k * W_COLS:(k + 1) * W_COLS], cols.bitcast(F32),
                                        ALU.subtract).then_inc(pairW_ready, 1)

            def split_hidden(n):
                dve.wait_ge(a_ready, n + 1)
                for q in (2, 3):
                    nc.vector.tensor_tensor(a_stack[q * E:q * E + R, :], H[0:R, bass.ds(n * CB, CB)],
                                            a_stack[0:R, :].bitcast(F32), ALU.subtract).then_inc(a_split, 1)

            def gate_blocks(k, slot, n):
                dve.wait_ge(b_done, n * NPAIR + k + 1)
                nc.vector.scalar_tensor_tensor(out=EVnext[:, 1, 2 * k:2 * k + 2, :], in0=Y[slot][:], scalar=0.0,
                                               in1=EVnext[:, 0, 2 * k:2 * k + 2, :], op0=ALU.max, op1=ALU.mult
                                               ).then_inc(vn_ready, 1)

            def low(J, n):
                whole = EVnext if J == 0 else EV
                for s in range(2):
                    dve.wait_ge(hi_ready, n * (2 * NB) + 2 * J + s + 1)
                    nc.vector.tensor_tensor(HL[:, J % 2, s, 1, :], whole[:, s, J, :],
                                            HL[:, J % 2, s, 0, :].bitcast(F32), ALU.subtract).then_inc(lo_ready, 1)

            def multiply(g, slot, n):
                J, _, full = groups[g]
                if full and g == min(k for k, (b, _, f) in enumerate(groups) if b == J and f):
                    dve.wait_ge(ev_in[J], n * 32 + 16)
                elif not full and g < last_of_block[J]:
                    dve.wait_ge(ev_in[J], n * 32 + 32)
                dve.wait_ge(y_done, n * NG + g + 1)
                dve.wait_ge(q_free, n * NG + g + 1)
                nc.vector.scalar_tensor_tensor(out=Q[:, g % Q_SLOTS, :, :], in0=Y[slot][:], scalar=pair_bias[:, g:g + 1],
                                               in1=EV[:, :, J, :], op0=ALU.add, op1=ALU.mult).then_inc(q_done, 1)

            def chunk(n, steps, prepare):
                for c, (kind, k) in enumerate(steps):
                    if kind == "gates":
                        gate_blocks(k, c % Y_SLOTS, n + 1)
                    elif kind == "group":
                        if k in SPLIT_AT:
                            low(SPLIT_AT[k], n)
                        if prepare and k == HIDDEN_AT:
                            split_hidden(n + 1)
                        if prepare and k == FIRST_SPLIT_AT:
                            low(0, n + 1)
                        multiply(k, c % Y_SLOTS, n)

            split_hidden(0)
            for k in range(NPAIR):
                gate_blocks(k, k, 0)
                if k == 0:
                    low(0, 0)
            dve.wait_ge(bias_in, 16)
            with dve.Fori(0, NCH - 1) as n:
                chunk(n, full_steps, True)
            chunk(NCH - 1, plain_steps, False)

            banks = [Y[n // 2][:, n % 2, :] for n in range(NCH)]
            dve.wait_ge(vectors_in, 16 * 3)
            for layer, (stat, sd, norm, stats, vec, width) in enumerate((
                    (stat1, sd1, norm1, stats1, vec1, M1), (stat2, sd2, norm2, stats2, vec2, M2))):
                for n in range(NCH):
                    if layer == 0:
                        dve.wait_ge(folded, n + 1)
                        nc.vector.bn_stats(stats[:, n, :], banks[n][0:M1, :]).then_inc(stat, 1)
                    else:
                        dve.wait_ge(lin2_done, n + 1)
                        nc.vector.tensor_scalar(lin2[:, n * CB:(n + 1) * CB], banks[n][0:M2, :], vec2[:, 0:1], None,
                                                ALU.add).then_inc(lin2_ready, 1)
                        dve.wait_ge(lin2_ready, n + 1)
                        nc.vector.bn_stats(stats[:, n, :], lin2[:, n * CB:(n + 1) * CB]).then_inc(stat, 1)
                col = [bn[0:width, layer, k:k + 1] for k in range(8)]
                dve.wait_ge(stat, NCH)
                nc.vector.bn_aggr(bn[0:width, layer, 0:2], stats[:].rearrange("p n k -> p (n k)")).then_inc(stat, 1)
                dve.wait_ge(stat, NCH + 1)
                nc.vector.tensor_scalar(col[2], col[1], BN_EPS, None, ALU.add).then_inc(stat, 1)
                dve.wait_ge(sd, 1)
                nc.vector.reciprocal(col[4], col[3]).then_inc(norm, 1)
                dve.wait_ge(norm, 1)
                nc.vector.tensor_tensor(col[5], col[4], vec[0:width, 1:2], ALU.mult).then_inc(norm, 1)
                dve.wait_ge(norm, 2)
                nc.vector.tensor_tensor(col[6], col[5], col[0], ALU.mult).then_inc(norm, 1)
                dve.wait_ge(norm, 3)
                nc.vector.tensor_tensor(col[7], vec[0:width, 2:3], col[6], ALU.subtract).then_inc(norm, 1)


_PLACED = ["pair_weights", "mlp_weights", "biases", "down", "up", "vectors1", "vectors2"]


def kernel(**inputs):
    import numpy as np
    import concourse.bacc as bacc
    from concourse.bass_utils import run_bass_kernel_spmd

    nc = bacc.Bacc("TRN2", target_bir_lowering=False, num_devices=1)
    given = {name.removeprefix("L0_rec_"): np.asarray(a) for name, a in inputs.items()}
    F, E = given["r_x"].shape[1], given["emb"].shape[1]
    placed = lay_out(F, E, *[given[n] for n in ("bl_W", "bl_b", "w1", "se_w1", "se_w2", "b1", "g1", "be1",
                                                "b2", "g2", "be2", "w3", "b3")])
    arrays, args = {}, []
    for name, a in [("x", given["r_x"]), ("emb", given["emb"]), ("w2", given["w2"])] + [(n, placed[n]) for n in _PLACED]:
        a = np.ascontiguousarray(a)
        arrays[f"in_{name}"] = a
        args.append(nc.dram_tensor(f"in_{name}", a.shape, mybir.dt.from_np(a.dtype), kind="ExternalInput").ap())
    out = nc.dram_tensor("out_prob", (arrays["in_x"].shape[0],), F32, kind="ExternalOutput").ap()
    build(nc, *args, out)
    r = run_bass_kernel_spmd(nc, [arrays], core_ids=[0])
    return r.results[0]["out_prob"]
```

```python
from contextlib import ExitStack

import concourse.bass as bass
from concourse import mybir

F32 = mybir.dt.float32
F32R = mybir.dt.float32r
I32 = mybir.dt.int32
ALU = mybir.AluOpType
ACT = mybir.ActivationFunctionType

PARTS = 128
FIELDS_PER_BLOCK = 4
STACK_SLOTS = 6
Q_SLOTS = 3
Y_SLOTS = 3
W_PIECES = 4
MLP_PIECES = 2
LATE_GROUPS = 4
ROWS_AT, ROWS_APART = 56, 0
HIDDEN_AT, HIDDEN_APART = 59, 2
GATES_AT, GATES_APART = 63, 1
FIRST_SPLIT_AT = 66
SPLIT_AT = {10: 1, 24: 2, 32: 3, 45: 4, 57: 5}
HIGH_LEAD = 6
CB = 512
BN_EPS = 1e-5


def plan_groups(F):
    nb = F // FIELDS_PER_BLOCK
    first = [i * F - i * (i + 1) // 2 for i in range(F)]

    def pair(i, j):
        return first[i] + j - i - 1

    groups, placed, tiles = [], [], 0

    def full_groups(i):
        nonlocal tiles
        for J in range(i // 4 + 1, nb):
            for q in range(4):
                placed.append((pair(i, 4 * J + q), tiles, q, len(groups)))
            groups.append((J, [(i, tiles)], True))
            tiles += 1

    for I in range(nb):
        i0, i1, i2, i3 = range(4 * I, 4 * I + 4)
        full_groups(i0)
        full_groups(i1)
        x_group = (I, [(i0, tiles), (i1, tiles + 1)], False)
        y_group = (I, [(i1, tiles + 2), (i2, tiles + 3)], False)
        first_tile, tiles = tiles, tiles + 4
        if I < nb - 1:
            x_at = len(groups)
            groups.append(x_group)
            full_groups(i2)
            y_at = len(groups)
            groups.append(y_group)
            full_groups(i3)
        else:
            y_at, x_at = len(groups), len(groups) + 1
            groups += [y_group, x_group]
        for q, j in ((1, i1), (2, i2), (3, i3)):
            placed.append((pair(i0, j), first_tile, q, x_at))
        placed.append((pair(i1, i3), first_tile + 1, 0, x_at))
        placed.append((pair(i1, i2), first_tile + 2, 2, y_at))
        placed.append((pair(i2, i3), first_tile + 3, 3, y_at))
    return groups, placed, tiles


def lay_out(F, E, bl_W, bl_b, w1, se_w1, se_w2, b1, g1, be1, w2, b2, g2, be2, w3, b3):
    import numpy as np

    groups, placed, tiles = plan_groups(F)
    M1, M2 = w1.shape[1], w3.shape[0]
    R = se_w1.shape[0]
    pair_weights = np.zeros((E, 4 * tiles, E), bl_W.dtype)
    mlp_weights = np.zeros((4, E, len(groups), 2, M1), w1.dtype)
    biases = np.zeros((4, E, len(groups)), bl_b.dtype)
    w1_of_pair = w1.reshape(2, -1, E, M1)
    for p, tile, q, g in placed:
        pair_weights[:, 4 * tile + q, :] = bl_W[p]
        mlp_weights[q, :, g, :, :] = w1_of_pair[:, p].transpose(1, 0, 2)
        biases[q, :, g] = bl_b[p]
    down = np.repeat(se_w1.T.reshape(-1, 4, R).transpose(1, 0, 2), E, axis=0)
    up = np.zeros((4, E, F * E), se_w2.dtype)
    up[:, 0:R, :] = np.repeat(se_w2.T, E, axis=1)
    vectors1 = np.zeros((PARTS, 3), b1.dtype)
    vectors1[0:M1] = np.stack([b1, g1, be1], axis=1)
    second = np.zeros((2, M1, 2, M2), w2.dtype)
    third = np.zeros((4, M2, 4), w3.dtype)
    for half in range(2):
        second[half, :, half, :] = w2
    for n in range(4):
        third[n, :, n] = w3[:, 0]
    vectors2 = np.tile(np.stack([b2, g2, be2, np.full_like(b2, b3[0])], axis=1), (2, 1))
    return {"pair_weights": pair_weights.reshape(E, -1), "mlp_weights": mlp_weights.reshape(PARTS, -1),
            "biases": biases.reshape(PARTS, -1), "down": down.reshape(PARTS, -1), "up": up.reshape(PARTS, -1),
            "vectors1": vectors1, "vectors2": vectors2,
            "second": second.reshape(PARTS, -1), "third": third.reshape(PARTS, -1)}


def build(nc, x, emb, pair_weights, mlp_weights, biases, down, up, vectors1, vectors2, second, third, out):
    B, F = x.shape
    rows, E = emb.shape
    vocab = (rows - 1) // F
    M1, M2 = second.shape[0] // 2, second.shape[1] // 2
    NB = F // FIELDS_PER_BLOCK
    R = down.shape[1] // NB
    NCH = B // CB
    TB = CB // PARTS
    assert E * FIELDS_PER_BLOCK == PARTS and M1 == 64 and M2 == 32 and B == 4 * CB

    groups, _, NT = plan_groups(F)
    NG = len(groups)
    NPAIR = NB // 2
    plain_steps = [("group", g) for g in range(NG)]
    full_steps = []
    for g in range(NG):
        full_steps += [("rows", k) for k in range(NPAIR) if g == ROWS_AT + k * ROWS_APART]
        full_steps += [("gates", k) for k in range(NPAIR) if g == GATES_AT + k * GATES_APART]
        full_steps.append(("group", g))
    assert len(full_steps) % Y_SLOTS == 0 and NG % Y_SLOTS == 0 and NG % Q_SLOTS == 0
    users = sorted({i for _, parts, _ in groups for i, _ in parts})
    slot_of = {i: k % STACK_SLOTS for k, i in enumerate(users)}
    per_slot = [len(users[s::STACK_SLOTS]) for s in range(STACK_SLOTS)]
    last_of_field = {i: max(g for g, (_, parts, _) in enumerate(groups) if i in [a for a, _ in parts]) for i in users}
    last_full_of_block = {J: max([g for g, (b, _, f) in enumerate(groups) if b == J and f], default=None)
                          for J in range(NB)}
    last_of_block = {J: max(g for g, (b, _, _) in enumerate(groups) if b == J) for J in range(NB)}
    first_of_field = {i: min(g for g, (_, parts, _) in enumerate(groups) if i in [a for a, _ in parts]) for i in users}

    with ExitStack() as ctx:
        def sb(name, shape, dt=F32):
            return ctx.enter_context(nc.sbuf_tensor(name, shape, dt))

        def ps(name, shape, dt=F32):
            return ctx.enter_context(nc.psum_tensor(name, shape, dt))

        def sem(name):
            return ctx.enter_context(nc.semaphore(name))

        pairW = sb("pairW", [PARTS, NT * PARTS], F32R)
        mlpW = sb("mlpW", [PARTS, NG, 2, M1])
        pair_bias = sb("pair_bias", [PARTS, NG])
        gate_down = sb("gate_down", [PARTS, NB, R])
        gate_up = sb("gate_up", [PARTS, F * E], F32R)
        ident = sb("ident", [PARTS, PARTS])
        w2s = sb("w2s", [PARTS, 2 * M2])
        w3s = sb("w3s", [PARTS, 4])
        vec1 = sb("vec1", [PARTS, 3])
        vec2 = sb("vec2", [2 * M2, 4])
        b3s = vec2[0:4, 3:4]
        EV_COLS = 2 * NB * CB
        work = sb("work", [PARTS, EV_COLS + B + Q_SLOTS * 2 * CB])
        raw = work[:, 0:NT * PARTS]
        EV = work[:, 0:EV_COLS].rearrange("p (s j b) -> p s j b", s=2, j=NB)
        H = work[:, EV_COLS:EV_COLS + B]
        Q = work[:, EV_COLS + B:EV_COLS + B + Q_SLOTS * 2 * CB].rearrange("p (k s b) -> p k s b", k=Q_SLOTS, s=2)
        EVnext = sb("EVnext", [PARTS, 2, NB, CB])
        HL = sb("HL", [PARTS, 2, 2, 2, CB], F32R)
        stack = sb("stack", [PARTS, STACK_SLOTS, 2, CB], F32R)
        nat = sb("nat", [PARTS, TB, F * E])
        a_stack = sb("a_stack", [PARTS, CB], F32R)
        up_raw = EVnext[:, 1, :, :].rearrange("p j b -> p (j b)")[:, 0:F * E]
        xs = sb("xs", [PARTS, B // PARTS, F], I32)
        field_base = sb("field_base", [PARTS, TB, F], I32)
        idx = sb("idx", [PARTS, TB, F], I32)
        stats1 = sb("stats1", [M1, NCH * 6])
        stats2 = sb("stats2", [2 * M2, NCH * 6])
        bn = sb("bn", [M1, 2, 8])
        act1 = nat[:, 0:2, :].rearrange("p t c -> p (t c)")[:, 0:2 * CB]
        act2 = nat[:, 2, 0:CB]
        lin2 = EVnext[0:2 * M2, 0, 0:2, :]
        probs = EVnext[0:4, 0, 2, :]
        v_sums_of_last = EVnext[0:M1, 1, NB - 1, :]

        Y = [ps(f"Y{k}", [PARTS, 2, CB]) for k in range(Y_SLOTS)]
        acc = ps("acc", [PARTS, CB])
        gate = ps("gate", [PARTS, CB])
        hidden_even, hidden_odd = gate[0:R, :], gate[PARTS // 2:PARTS // 2 + R, :]

        names = ("x_in base_done idx_done idx_seen ident_clear ident_done a_clear up_in hi_up up_ready "
                 "down_in hi_w pairW_ready mlpW_in bias_in vectors_in t_done en_ready z_done z_even z_summed a_high a_ready a_split b_done vn_ready "
                 "hi_ready lo_ready y_done q_done q_free acc_free v_moved h_ready stats_taken stat1 norm1 sd1 act1_done lin2_done lin2_ready "
                 "first_e_in first_v act_seen stat2 norm2 sd2 act2_done out_lin prob_done stored").split()
        S = {n: sem(n) for n in names}
        (x_in, base_done, idx_done, idx_seen, ident_clear, ident_done, a_clear, up_in, hi_up, up_ready,
         down_in, hi_w, pairW_ready, mlpW_in, bias_in, vectors_in, t_done, en_ready, z_done, z_even, z_summed, a_high, a_ready, a_split, b_done, vn_ready,
         hi_ready, lo_ready, y_done, q_done, q_free, acc_free, v_moved, h_ready, stats_taken, stat1, norm1, sd1, act1_done, lin2_done,
         lin2_ready, first_e_in, first_v, act_seen, stat2, norm2, sd2, act2_done, out_lin, prob_done, stored) = [S[n] for n in names]
        w_in = [sem(f"w_in{k}") for k in range(W_PIECES)]
        gathered = [sem(f"gathered{J}") for J in range(NB)]
        ev_in = [sem(f"ev_in{J}") for J in range(NB)]
        stack_in = [sem(f"stack_in{s}") for s in range(STACK_SLOTS)]

        def stack_landed(i, n):
            return (n * per_slot[slot_of[i]] + users.index(i) // STACK_SLOTS + 1) * 64

        W_COLS = NT * PARTS // W_PIECES
        xv = x.rearrange("(t p) f -> p t f", p=PARTS)
        block = ctx.enter_context(nc.Block())

        @block.sync
        def _(sp):
            sp.dma_start(xs[:], xv).then_inc(x_in, 16)
            sp.dma_start(up_raw, up).then_inc(up_in, 16)
            for k in range(W_PIECES):
                for q in range(4):
                    sp.dma_start(raw[q * E:(q + 1) * E, k * W_COLS:(k + 1) * W_COLS],
                                 pair_weights[:, k * W_COLS:(k + 1) * W_COLS]).then_inc(w_in[k], 16)
            sp.dma_start(gate_down[:].rearrange("p j r -> p (j r)"), down).then_inc(down_in, 16)
            sp.dma_start(pair_bias[:], biases).then_inc(bias_in, 16)
            mlpW_rows = mlpW[:].rearrange("p g a m -> p (g a m)")
            for k in range(MLP_PIECES):
                cols = slice(k * NG * 2 * M1 // MLP_PIECES, (k + 1) * NG * 2 * M1 // MLP_PIECES)
                sp.dma_start(mlpW_rows[:, cols], mlp_weights[:, cols]).then_inc(mlpW_in, 16)
            sp.dma_start(vec1[:], vectors1).then_inc(vectors_in, 16)
            sp.dma_start(vec2[:], vectors2).then_inc(vectors_in, 16)
            sp.dma_start(w2s[:], second).then_inc(vectors_in, 16)
            sp.dma_start(w3s[:], third).then_inc(vectors_in, 16)

            def value(v):
                return v if isinstance(v, int) else sp.to_reg(v)

            def swap(J, n):
                landed = value(n * 32 + 16)
                split = value(n * (2 * NB) + 2 * J + 2)
                read = value(n * NG + (last_full_of_block[J] or 0) + 1)
                sp.wait_ge(ev_in[J], landed)
                if J >= 1:
                    sp.wait_ge(lo_ready, split)
                if last_full_of_block[J] is not None:
                    sp.wait_ge(q_done, read)
                sp.dma_start(EV[0:E, :, J, :], EV[3 * E:4 * E, :, J, :]).then_inc(ev_in[J], 16)

            def feed(n, is_first):
                def take(J):
                    made = value(n * NPAIR + J // 2 + 1)
                    read = value((n - 1) * NG + last_of_block[J] + 1)
                    sp.wait_ge(vn_ready, made)
                    if not is_first:
                        sp.wait_ge(q_done, read)
                    if is_first:
                        sp.dma_start(EV[:, 1, J, :], EVnext[:, 1, J, :]).then_inc(ev_in[J], 16)
                    else:
                        sp.dma_start(EV[:, :, J, :], EVnext[:, :, J, :]).then_inc(ev_in[J], 16)

                def build_stack(i):
                    I, r, slot = i // 4, i % 4, slot_of[i]
                    split = value(n * (2 * NB) + 2 * I + 2)
                    sharing = users[slot::STACK_SLOTS]
                    k = sharing.index(i)
                    if k:
                        through = value(n * NG + last_of_field[sharing[k - 1]] + 1)
                    elif not is_first:
                        through = value((n - 1) * NG + last_of_field[sharing[-1]] + 1)
                    sp.wait_ge(lo_ready, split)
                    if k or not is_first:
                        sp.wait_ge(y_done, through)
                    for q in range(4):
                        sp.dma_start(stack[q * E:(q + 1) * E, slot, :, :].bitcast(F32),
                                     HL[r * E:(r + 1) * E, I % 2, :, q % 2, :].bitcast(F32)).then_inc(stack_in[slot], 16)

                if is_first:
                    sp.wait_ge(pairW_ready, W_PIECES)
                    for k in range(NPAIR):
                        sp.wait_ge(en_ready, k + 1)
                        sp.dma_start(EV[:, 0, 2 * k:2 * k + 2, :], EVnext[:, 0, 2 * k:2 * k + 2, :]
                                     ).then_inc(first_e_in, 16)
                    sp.wait_ge(first_e_in, 16 * NPAIR)
                build_stack(users[0])
                take(1)
                if not is_first:
                    swap(NB - 1, n - 1)
                for J in range(2, NB):
                    take(J)
                build_stack(users[1])
                take(0)
                swap(0, n)
                later = [(last_of_field[users[k - STACK_SLOTS]] if k >= STACK_SLOTS else 0, build_stack, (i,))
                         for k, i in enumerate(users) if k >= 2]
                later += [(last_full_of_block[J], swap, (J, n)) for J in range(1, NB - 1)]
                for _, move, which in sorted(later, key=lambda m: m[0]):
                    move(*which)

            feed(0, True)
            with sp.Fori(1, NCH) as n:
                feed(n, False)
            swap(NB - 1, NCH - 1)
            sp.wait_ge(prob_done, 1)
            sp.dma_start(out.rearrange("(n b) -> n b", b=CB), probs).then_inc(stored, 16)
            sp.wait_ge(stored, 16)

        @block.gpsimd
        def _(pool):
            nc.gpsimd.iota(field_base[:], pattern=[[0, TB], [vocab, F]], base=0, channel_multiplier=0
                           ).then_inc(base_done, 1)
            pool.wait_ge(ident_clear, 1)
            nc.gpsimd.affine_select(out=ident[:], in_=ident[:], compare_op=ALU.not_equal, fill=1.0, base=0,
                                    pattern=[[-1, PARTS]], channel_multiplier=1).then_inc(ident_done, 1)
            pool.wait_ge(base_done, 1)
            pool.wait_ge(x_in, 16)

            def gather(n, is_first):
                if not is_first:
                    for J in range(NB):
                        pool.wait_ge(gathered[J], n * (16 * FIELDS_PER_BLOCK * TB))
                    pool.wait_ge(t_done, n * NPAIR)
                nc.gpsimd.tensor_tensor(idx[:], xs[:, bass.ds(n * TB, TB), :], field_base[:], ALU.add
                                        ).then_inc(idx_done, 1)
                pool.wait_ge(idx_done, n + 1)
                pool.sem_inc(idx_seen, 1)
                for J in range(NB):
                    for t in range(TB):
                        for f in range(FIELDS_PER_BLOCK * J, FIELDS_PER_BLOCK * (J + 1)):
                            nc.gpsimd.indirect_dma_start(
                                nat[:, t, f * E:(f + 1) * E], None, emb,
                                bass.IndirectOffsetOnAxis(ap=idx[:, t, f:f + 1], axis=0)).then_inc(gathered[J], 16)

            gather(0, True)
            with pool.Fori(1, NCH) as n:
                gather(n, False)

        @block.tensor
        def _(pe):
            def fill_rows(k, slot, n):
                for J in (2 * k, 2 * k + 1):
                    pe.wait_ge(gathered[J], (n + 1) * (16 * FIELDS_PER_BLOCK * TB))
                    for t in range(TB):
                        mm = nc.tensor.transpose(Y[slot][:, J % 2, t * PARTS:(t + 1) * PARTS],
                                                 nat[:, t, J * PARTS:(J + 1) * PARTS], ident[:])
                mm.then_inc(t_done, 1)

            def gate_hidden(k, n, is_first):
                pe.wait_ge(en_ready, n * NPAIR + k + 1)
                if k == 0 and not is_first:
                    pe.wait_ge(z_summed, n)
                for J, sums in ((2 * k, hidden_even), (2 * k + 1, hidden_odd)):
                    mm = nc.tensor.matmul(sums, gate_down[:, J, :], EVnext[:, 0, J, :],
                                          start=(k == 0), stop=(k == NPAIR - 1))
                if k == NPAIR - 1:
                    mm.then_inc(z_done, 1)

            def fill_gates(k, slot, n):
                if k == 0:
                    pe.wait_ge(a_split, 2 * n + 2)
                for J in (2 * k, 2 * k + 1):
                    mm = nc.tensor.matmul(Y[slot][:, J % 2, :], gate_up[:, J * PARTS:(J + 1) * PARTS], a_stack[:],
                                          start=True, stop=True)
                mm.then_inc(b_done, 1)

            def fill_products(g, slot, n):
                _, parts, _ = groups[g]
                for i, _ in parts:
                    if g == first_of_field[i]:
                        pe.wait_ge(stack_in[slot_of[i]], stack_landed(i, n))
                for s in range(2):
                    for k, (i, tile) in enumerate(parts):
                        mm = nc.tensor.matmul(Y[slot][:, s, :], pairW[:, tile * PARTS:(tile + 1) * PARTS],
                                              stack[:, slot_of[i], s, :],
                                              start=(k == 0), stop=(k == len(parts) - 1))
                mm.then_inc(y_done, 1)

            def contract(g, n):
                if g == 0:
                    pe.wait_ge(acc_free, n + 1)
                for s in range(2):
                    mm = nc.tensor.matmul(acc[s * M1:(s + 1) * M1, :], mlpW[:, g, s, :], Q[:, g % Q_SLOTS, s, :],
                                          start=(g == 0), stop=(g == NG - 1))
                mm.then_inc(q_free, 1)

            def chunk(n, steps, prepare):
                for c, (kind, k) in enumerate(steps):
                    if kind == "group":
                        pe.wait_ge(q_done, n * NG + k + 1)
                    elif kind == "rows":
                        pe.wait_ge(en_ready, (n + 1) * NPAIR + k + 1)
                    else:
                        pe.wait_ge(vn_ready, (n + 1) * NPAIR + k + 1)
                    slot, ahead = c % Y_SLOTS, c + Y_SLOTS
                    if ahead < len(steps):
                        kind_ahead, k_ahead = steps[ahead]
                        if kind_ahead == "group":
                            fill_products(k_ahead, slot, n)
                        elif kind_ahead == "rows":
                            fill_rows(k_ahead, slot, n + 1)
                        else:
                            fill_gates(k_ahead, slot, n + 1)
                    elif prepare:
                        fill_products(ahead - len(steps), slot, n + 1)
                    if kind == "group":
                        contract(k, n)
                    elif kind == "rows":
                        gate_hidden(k, n + 1, False)

            pe.sem_inc(q_free, Q_SLOTS)
            pe.sem_inc(acc_free, 1)
            pe.wait_ge(ident_done, 1)
            pe.wait_ge(down_in, 16)
            for k in range(NPAIR):
                fill_rows(k, k, 0)
                if k:
                    gate_hidden(k - 1, 0, True)
            gate_hidden(NPAIR - 1, 0, True)
            pe.wait_ge(up_ready, 2)
            for k in range(NPAIR):
                fill_gates(k, k, 0)
            pe.wait_ge(pairW_ready, W_PIECES)
            for k in range(NPAIR):
                pe.wait_ge(vn_ready, k + 1)
                fill_products(k, k, 0)
            pe.wait_ge(mlpW_in, 16 * MLP_PIECES)
            with pe.Fori(0, NCH - 1) as n:
                chunk(n, full_steps, True)
            chunk(NCH - 1, plain_steps, False)

            pe.wait_ge(vectors_in, 16 * 4)
            for k in range(2):
                pe.wait_ge(act1_done, 2 * k + 2)
                nc.tensor.matmul(Y[k][0:2 * M2, 0, :], w2s[:], act1[:, k * CB:(k + 1) * CB],
                                 start=True, stop=True).then_inc(lin2_done, 1)
            pe.wait_ge(act2_done, 2)
            nc.tensor.matmul(Y[2][0:4, 0, :], w3s[:], act2, start=True, stop=True).then_inc(out_lin, 1)

        @block.scalar
        def _(act):
            act.wait_ge(up_in, 16)
            nc.scalar.copy(gate_up[:], up_raw).then_inc(hi_up, 1)
            for k in range(W_PIECES):
                act.wait_ge(w_in[k], 16 * 4)
                nc.scalar.copy(pairW[:, k * W_COLS:(k + 1) * W_COLS], raw[:, k * W_COLS:(k + 1) * W_COLS]
                               ).then_inc(hi_w, 1)

            def take_rows(k, slot, n, is_first):
                act.wait_ge(t_done, n * NPAIR + k + 1)
                if not is_first:
                    for J in (2 * k, 2 * k + 1):
                        act.wait_ge(ev_in[J], n * 32 - 16)
                    if k == 0:
                        act.wait_ge(lo_ready, (n - 1) * (2 * NB) + 2)
                nc.scalar.copy(EVnext[:, 0, 2 * k:2 * k + 2, :], Y[slot][:]).then_inc(en_ready, 1)

            def hidden(n, is_first):
                act.wait_ge(z_done, n + 1)
                if is_first:
                    act.wait_ge(pairW_ready, W_PIECES)
                    act.wait_ge(a_clear, 1)
                else:
                    act.wait_ge(b_done, n * NPAIR)
                nc.scalar.copy(H[0:R, bass.ds(n * CB, CB)], hidden_even).then_inc(z_even, 1)
                act.wait_ge(z_summed, n + 1)
                act.sem_inc(act_seen, 1)
                whole = H[0:R, bass.ds(n * CB, CB)]
                for q in range(2):
                    part = nc.scalar.activation(a_stack[q * E:q * E + R, :], whole, ACT.Relu, scale=1.0 / E)
                part.then_inc(a_high, 1)
                act.wait_ge(a_high, n + 1)
                act.sem_inc(act_seen, 1)
                nc.scalar.activation(whole, whole, ACT.Relu, scale=1.0 / E).then_inc(a_ready, 1)

            def high(J, n, kinds=(0, 1)):
                if J == 1:
                    act.wait_ge(y_done, n * NG + 1)
                elif J >= 2:
                    for i in users:
                        if i // 4 == J - 2:
                            act.wait_ge(stack_in[slot_of[i]], stack_landed(i, n))
                if J >= 1:
                    act.wait_ge(ev_in[J], n * 32 + 16)
                whole = EVnext if J == 0 else EV
                for s in kinds:
                    if J == 0:
                        act.wait_ge(vn_ready if s else en_ready, n * NPAIR + 1)
                    nc.scalar.copy(HL[:, J % 2, s, 0, :], whole[:, s, J, :]).then_inc(hi_ready, 1)

            def chunk(n, steps, prepare):
                for c, (kind, k) in enumerate(steps):
                    if kind == "rows":
                        take_rows(k, c % Y_SLOTS, n + 1, False)
                    elif kind == "group":
                        for split, J in SPLIT_AT.items():
                            if k == max(0, split - HIGH_LEAD):
                                high(J, n)
                        if prepare and k == HIDDEN_AT:
                            hidden(n + 1, False)
                        if prepare and k == FIRST_SPLIT_AT:
                            for i in users:
                                if i // 4 == NB - 2:
                                    act.wait_ge(stack_in[slot_of[i]], stack_landed(i, n))
                            high(0, n + 1)
                act.wait_ge(q_free, n * NG + NG + Q_SLOTS)
                nc.scalar.activation(H[:, bass.ds(n * CB, CB)], acc[:], ACT.Identity, bias=vec1[:, 0:1]
                                     ).then_inc(acc_free, 1)
                act.wait_ge(acc_free, n + 2)
                beside = H[0:M1, bass.ds((n + 1) * CB, CB)] if prepare else v_sums_of_last
                nc.scalar.copy(beside, H[M1:2 * M1, bass.ds(n * CB, CB)]).then_inc(v_moved, 1)

            take_rows(0, 0, 0, True)
            high(0, 0, (0,))
            for k in range(1, NPAIR):
                take_rows(k, k, 0, True)
            hidden(0, True)
            act.wait_ge(first_v, 1)
            nc.scalar.copy(HL[:, 0, 1, 0, :], EVnext[:, 1, 0, :]).then_inc(hi_ready, 1)
            act.wait_ge(vectors_in, 16 * 4)
            with act.Fori(0, NCH - 1) as n:
                chunk(n, full_steps, True)
            chunk(NCH - 1, plain_steps, False)

            def take_root(layer, stat, sd, width):
                act.wait_ge(stat, 2)
                nc.scalar.activation(bn[0:width, layer, 3:4], bn[0:width, layer, 2:3], ACT.Sqrt).then_inc(sd, 1)

            take_root(0, stat1, sd1, M1)
            act.wait_ge(norm1, 4)
            for n in range(NCH):
                nc.scalar.activation(act1[n % 2 * M1:(n % 2 + 1) * M1, n // 2 * CB:(n // 2 + 1) * CB],
                                     H[0:M1, n * CB:(n + 1) * CB], ACT.Relu,
                                     scale=bn[0:M1, 0, 5:6], bias=bn[0:M1, 0, 7:8]).then_inc(act1_done, 1)
            for k in range(2):
                act.wait_ge(lin2_done, k + 1)
                nc.scalar.activation(lin2[:, k, :], Y[k][0:2 * M2, 0, :], ACT.Identity, bias=vec2[:, 0:1]
                                     ).then_inc(lin2_ready, 1)
            take_root(1, stat2, sd2, 2 * M2)
            act.wait_ge(norm2, 4)
            for k in range(2):
                nc.scalar.activation(act2[k * 2 * M2:(k + 1) * 2 * M2, :], lin2[:, k, :], ACT.Relu,
                                     scale=bn[0:2 * M2, 1, 5:6], bias=bn[0:2 * M2, 1, 7:8]).then_inc(act2_done, 1)
            act.wait_ge(out_lin, 1)
            nc.scalar.activation(probs, Y[2][0:4, 0, :], ACT.Sigmoid, bias=b3s).then_inc(prob_done, 1)

        @block.vector
        def _(dve):
            nc.vector.memset(ident[:], 0.0).then_inc(ident_clear, 1)
            nc.vector.memset(a_stack[:].bitcast(F32), 0.0).then_inc(a_clear, 1)
            dve.wait_ge(hi_up, 1)
            for q in (1, 3):
                rows = gate_up[q * E:(q + 1) * E, :]
                nc.vector.tensor_tensor(rows, up_raw[q * E:(q + 1) * E, :], rows.bitcast(F32), ALU.subtract
                                        ).then_inc(up_ready, 1)
            for k in range(W_PIECES):
                dve.wait_ge(hi_w, k + 1)
                cols = pairW[2 * E:4 * E, k * W_COLS:(k + 1) * W_COLS]
                nc.vector.tensor_tensor(cols, raw[2 * E:4 * E, k * W_COLS:(k + 1) * W_COLS], cols.bitcast(F32),
                                        ALU.subtract).then_inc(pairW_ready, 1)

            def sum_hidden(n):
                dve.wait_ge(z_even, n + 1)
                whole = H[0:R, bass.ds(n * CB, CB)]
                nc.vector.tensor_tensor(whole, hidden_odd, whole, ALU.add).then_inc(z_summed, 1)

            def split_hidden(n):
                dve.wait_ge(a_ready, n + 1)
                for q in (2, 3):
                    nc.vector.tensor_tensor(a_stack[q * E:q * E + R, :], H[0:R, bass.ds(n * CB, CB)],
                                            a_stack[0:R, :].bitcast(F32), ALU.subtract).then_inc(a_split, 1)

            def gate_blocks(k, slot, n):
                dve.wait_ge(b_done, n * NPAIR + k + 1)
                nc.vector.scalar_tensor_tensor(out=EVnext[:, 1, 2 * k:2 * k + 2, :], in0=Y[slot][:], scalar=0.0,
                                               in1=EVnext[:, 0, 2 * k:2 * k + 2, :], op0=ALU.max, op1=ALU.mult
                                               ).then_inc(vn_ready, 1)

            def low(J, n, kinds=(0, 1)):
                whole = EVnext if J == 0 else EV
                for s in kinds:
                    dve.wait_ge(hi_ready, n * (2 * NB) + 2 * J + s + 1)
                    nc.vector.tensor_tensor(HL[:, J % 2, s, 1, :], whole[:, s, J, :],
                                            HL[:, J % 2, s, 0, :].bitcast(F32), ALU.subtract).then_inc(lo_ready, 1)

            def multiply(g, slot, n):
                J, parts, full = groups[g]
                is_y = not full and parts[0][0] % FIELDS_PER_BLOCK == 1
                if full and g == min(k for k, (b, _, f) in enumerate(groups) if b == J and f):
                    dve.wait_ge(ev_in[J], n * 32 + 16)
                elif not full and not is_y:
                    dve.wait_ge(ev_in[J], n * 32 + 32)
                dve.wait_ge(y_done, n * NG + g + 1)
                dve.wait_ge(q_free, n * NG + g + 1)
                rows = slice(2 * E if is_y else 0, PARTS)
                nc.vector.scalar_tensor_tensor(out=Q[rows, g % Q_SLOTS, :, :], in0=Y[slot][rows], scalar=pair_bias[rows, g:g + 1],
                                               in1=EV[rows, :, J, :], op0=ALU.add, op1=ALU.mult).then_inc(q_done, 1)

            def sum_chunk(n, is_last):
                dve.wait_ge(v_moved, n + 1)
                beside = v_sums_of_last if is_last else H[0:M1, bass.ds((n + 1) * CB, CB)]
                nc.vector.tensor_tensor(H[0:M1, bass.ds(n * CB, CB)], H[0:M1, bass.ds(n * CB, CB)], beside, ALU.add
                                        ).then_inc(h_ready, 1)

            def chunk_stats(n):
                dve.wait_ge(h_ready, n + 1)
                nc.vector.bn_stats(stats1[:, bass.ds(n * 6, 6)], H[0:M1, bass.ds(n * CB, CB)]).then_inc(stats_taken, 1)

            def chunk(n, steps, prepare):
                for c, (kind, k) in enumerate(steps):
                    if kind == "gates":
                        gate_blocks(k, c % Y_SLOTS, n + 1)
                    elif kind == "group" and k >= LATE_GROUPS:
                        if k in SPLIT_AT:
                            low(SPLIT_AT[k], n)
                        if prepare and k == HIDDEN_AT:
                            sum_hidden(n + 1)
                        if prepare and k == HIDDEN_AT + HIDDEN_APART:
                            split_hidden(n + 1)
                        if prepare and k == FIRST_SPLIT_AT:
                            low(0, n + 1)
                        multiply(k, c % Y_SLOTS, n)
                if prepare:
                    for g in range(LATE_GROUPS - 1):
                        multiply(g, g % Y_SLOTS, n + 1)
                sum_chunk(n, not prepare)
                if prepare:
                    multiply(LATE_GROUPS - 1, (LATE_GROUPS - 1) % Y_SLOTS, n + 1)
                chunk_stats(n)

            low(0, 0, (0,))
            sum_hidden(0)
            split_hidden(0)
            dve.wait_ge(b_done, 1)
            for J, done in ((0, first_v), (1, vn_ready)):
                nc.vector.scalar_tensor_tensor(out=EVnext[:, 1, J, :], in0=Y[0][:, J, :], scalar=0.0,
                                               in1=EVnext[:, 0, J, :], op0=ALU.max, op1=ALU.mult).then_inc(done, 1)
            low(0, 0, (1,))
            for k in range(1, NPAIR):
                gate_blocks(k, k, 0)
            dve.wait_ge(bias_in, 16)
            for g in range(LATE_GROUPS):
                multiply(g, g % Y_SLOTS, 0)
            with dve.Fori(0, NCH - 1) as n:
                chunk(n, full_steps, True)
            chunk(NCH - 1, plain_steps, False)

            dve.wait_ge(vectors_in, 16 * 4)
            for layer, (stat, sd, norm, stats, vec, width) in enumerate((
                    (stat1, sd1, norm1, stats1, vec1, M1), (stat2, sd2, norm2, stats2, vec2, 2 * M2))):
                if layer == 1:
                    for k in range(2):
                        dve.wait_ge(lin2_ready, k + 1)
                        nc.vector.bn_stats(stats[:, k * 6:(k + 1) * 6], lin2[:, k, :]).then_inc(stats_taken, 1)
                    dve.wait_ge(stats_taken, NCH + 2)
                    for half in range(2):
                        nc.vector.tensor_copy(stats[half * M2:(half + 1) * M2, 12:24],
                                              stats[(1 - half) * M2:(2 - half) * M2, 0:12]).then_inc(stats_taken, 1)
                col = [bn[0:width, layer, k:k + 1] for k in range(8)]
                dve.wait_ge(stats_taken, (layer + 1) * NCH)
                nc.vector.bn_aggr(bn[0:width, layer, 0:2], stats[:]).then_inc(stat, 1)
                dve.wait_ge(stat, 1)
                nc.vector.tensor_scalar(col[2], col[1], BN_EPS, None, ALU.add).then_inc(stat, 1)
                dve.wait_ge(sd, 1)
                nc.vector.reciprocal(col[4], col[3]).then_inc(norm, 1)
                dve.wait_ge(norm, 1)
                nc.vector.tensor_tensor(col[5], col[4], vec[0:width, 1:2], ALU.mult).then_inc(norm, 1)
                dve.wait_ge(norm, 2)
                nc.vector.tensor_tensor(col[6], col[5], col[0], ALU.mult).then_inc(norm, 1)
                dve.wait_ge(norm, 3)
                nc.vector.tensor_tensor(col[7], vec[0:width, 2:3], col[6], ALU.subtract).then_inc(norm, 1)


_PLACED = ["pair_weights", "mlp_weights", "biases", "down", "up", "vectors1", "vectors2", "second", "third"]


def kernel(**inputs):
    import numpy as np
    import concourse.bacc as bacc
    from concourse.bass_utils import run_bass_kernel_spmd

    nc = bacc.Bacc("TRN2", target_bir_lowering=False, num_devices=1)
    given = {name.removeprefix("L0_rec_"): np.asarray(a) for name, a in inputs.items()}
    F, E = given["r_x"].shape[1], given["emb"].shape[1]
    placed = lay_out(F, E, *[given[n] for n in ("bl_W", "bl_b", "w1", "se_w1", "se_w2", "b1", "g1", "be1",
                                                "w2", "b2", "g2", "be2", "w3", "b3")])
    arrays, args = {}, []
    for name, a in [("x", given["r_x"]), ("emb", given["emb"])] + [(n, placed[n]) for n in _PLACED]:
        a = np.ascontiguousarray(a)
        arrays[f"in_{name}"] = a
        args.append(nc.dram_tensor(f"in_{name}", a.shape, mybir.dt.from_np(a.dtype), kind="ExternalInput").ap())
    out = nc.dram_tensor("out_prob", (arrays["in_x"].shape[0],), F32, kind="ExternalOutput").ap()
    build(nc, *args, out)
    r = run_bass_kernel_spmd(nc, [arrays], core_ids=[0])
    return r.results[0]["out_prob"]
```
